# Optimizing a Trainium2 kernel written in Bass

```python
import numpy as np
import jax
import jax.numpy as jnp

def _softmax(x, axis=-1):
    return jax.nn.softmax(x, axis=axis)

def _gelu(x):
    return jax.nn.gelu(x, approximate=True)

def _silu(x):
    return jax.nn.silu(x)

def _sigmoid(x):
    return jax.nn.sigmoid(x)

def _layernorm(x, axis=-1, eps=1e-05):
    m = jnp.mean(x, axis=axis, keepdims=True)
    v = jnp.var(x, axis=axis, keepdims=True)
    return (x - m) / jnp.sqrt(v + eps)

def _scatter_add(tgt, idx, src, axis=0):
    return tgt.at[idx].add(src)

def _segment_sum(src, seg, n):
    return jax.ops.segment_sum(src, seg, n)
kernel_name = 'mk_macaron_d1_jaxref_r4_f7536b'

def setup_inputs(seed: int=0):
    np.random.seed(seed)
    _w = jnp.asarray

    def _L0_attn_setup():
        import jax, jax.numpy as jnp
        import numpy as np
        D_MODEL = 256
        D_STATE = 64
        D_HEAD = 64
        N_HEADS = 16
        D_INNER = D_HEAD * N_HEADS
        K = 4
        BATCH = 4
        SEQ = 1024
        LN_EPS = 1e-05

        def _ssd_scan(xh, Bm, Cm, A_param):
            A_disc = jnp.exp(-jnp.exp(A_param))

            def step(h, inp):
                x_t, B_t, C_t = inp
                h = h * A_disc + B_t[:, None, None, :] * x_t[..., None]
                y_t = jnp.einsum('bhdn,bn->bhd', h, C_t)
                return (h, y_t)
            b = xh.shape[0]
            h0 = jnp.zeros((b, N_HEADS, D_HEAD, D_STATE), xh.dtype)
            xs = (jnp.swapaxes(xh, 0, 1), jnp.swapaxes(Bm, 0, 1), jnp.swapaxes(Cm, 0, 1))
            _, ys = jax.lax.scan(step, h0, xs)
            return jnp.swapaxes(ys, 0, 1)
        key = jax.random.key(seed)
        k0, k1, k2, k3, k4 = jax.random.split(key, 5)
        x = jax.random.normal(k0, (BATCH, SEQ, D_MODEL), jnp.float32)
        in_proj_w = jax.random.normal(k1, (2 * D_INNER + 2 * D_STATE, D_MODEL), jnp.float32) / np.sqrt(D_MODEL).astype(np.float32)
        conv_w = jax.random.normal(k2, (D_INNER, 1, K), jnp.float32) * 0.5
        conv_b = jax.random.normal(k3, (D_INNER,), jnp.float32) * 0.1
        A_param = jnp.broadcast_to(-jnp.log(jnp.arange(1, D_STATE + 1, dtype=jnp.float32))[None, None, :], (N_HEADS, D_HEAD, D_STATE))
        ln_w = jnp.ones((D_INNER,), jnp.float32)
        ln_b = jnp.zeros((D_INNER,), jnp.float32)
        out_proj_w = jax.random.normal(k4, (D_MODEL, D_INNER), jnp.float32) / np.sqrt(D_INNER).astype(np.float32)
        return {'x': x, 'in_proj_w': in_proj_w, 'conv_w': conv_w, 'conv_b': conv_b, 'A_param': A_param, 'ln_w': ln_w, 'ln_b': ln_b, 'out_proj_w': out_proj_w}
    _L0_attn_in = _L0_attn_setup()

    def _L0_ffn_setup():
        import jax, jax.numpy as jnp
        import numpy as np
        B, S, H = (1, 512, 256)
        E, K = (16, 4)
        G, TG = (4, 2)
        I_MOE = 128
        N_SH = 2
        SCALE = 2.5

        def _mlp(x, gw, uw, dw):
            return jax.nn.silu(x @ gw.T) * (x @ uw.T) @ dw.T

        def _route(x2d, router_weight, e_bias):
            T = x2d.shape[0]
            scores = jax.nn.sigmoid(x2d @ router_weight.T)
            sc = scores + e_bias[None, :]
            group_scores = jnp.sum(jax.lax.top_k(sc.reshape(T, G, E // G), 2)[0], axis=-1)
            _, gidx = jax.lax.top_k(group_scores, TG)
            gmask = jnp.zeros((T, G), sc.dtype).at[jnp.arange(T)[:, None], gidx].set(1.0)
            smask = jnp.repeat(gmask, E // G, axis=1)
            masked = jnp.where(smask > 0, sc, 0.0)
            _, tidx = jax.lax.top_k(masked, K)
            tw = jnp.take_along_axis(scores, tidx, axis=1)
            tw = tw / (jnp.sum(tw, axis=-1, keepdims=True) + 1e-20)
            tw = tw * SCALE
            return (tidx, tw)

        def _moe_forward(hidden_states, router_weight, e_bias, gate_w, up_w, down_w, sh_gate_w, sh_up_w, sh_down_w):
            orig_shape = hidden_states.shape
            x = hidden_states.reshape(-1, H)
            T = x.shape[0]
            tidx, tw = _route(x, router_weight, e_bias)
            g = jnp.einsum('th,eih->tei', x, gate_w)
            u = jnp.einsum('th,eih->tei', x, up_w)
            h = jax.nn.silu(g) * u
            yo = jnp.einsum('tei,ehi->teh', h, down_w)
            combine = jnp.zeros((T, E), tw.dtype).at[jnp.arange(T)[:, None], tidx].add(tw)
            routed = jnp.einsum('te,teh->th', combine, yo)
            shared = _mlp(hidden_states.reshape(-1, H), sh_gate_w, sh_up_w, sh_down_w)
            return (routed + shared).reshape(orig_shape)
        key = jax.random.key(seed)
        ks = jax.random.split(key, 9)
        s = 0.02
        return {'hidden_states': jax.random.normal(ks[0], (B, S, H), jnp.float32), 'router_weight': jax.random.normal(ks[1], (E, H), jnp.float32) * s, 'e_bias': jnp.zeros((E,), jnp.float32), 'gate_w': jax.random.normal(ks[2], (E, I_MOE, H), jnp.float32) * s, 'up_w': jax.random.normal(ks[3], (E, I_MOE, H), jnp.float32) * s, 'down_w': jax.random.normal(ks[4], (E, H, I_MOE), jnp.float32) * s, 'sh_gate_w': jax.random.normal(ks[5], (N_SH * I_MOE, H), jnp.float32) * s, 'sh_up_w': jax.random.normal(ks[6], (N_SH * I_MOE, H), jnp.float32) * s, 'sh_down_w': jax.random.normal(ks[7], (H, N_SH * I_MOE), jnp.float32) * s}
    _L0_ffn_in = _L0_ffn_setup()
    _d = {'L0_attn_x': _L0_attn_in['x'], 'L0_attn_in_proj_w': _L0_attn_in['in_proj_w'], 'L0_attn_conv_w': _L0_attn_in['conv_w'], 'L0_attn_conv_b': _L0_attn_in['conv_b'], 'L0_attn_A_param': _L0_attn_in['A_param'], 'L0_attn_ln_w': _L0_attn_in['ln_w'], 'L0_attn_ln_b': _L0_attn_in['ln_b'], 'L0_attn_out_proj_w': _L0_attn_in['out_proj_w'], 'L0_ffn_router_weight': _L0_ffn_in['router_weight'], 'L0_ffn_e_bias': _L0_ffn_in['e_bias'], 'L0_ffn_gate_w': _L0_ffn_in['gate_w'], 'L0_ffn_up_w': _L0_ffn_in['up_w'], 'L0_ffn_down_w': _L0_ffn_in['down_w'], 'L0_ffn_sh_gate_w': _L0_ffn_in['sh_gate_w'], 'L0_ffn_sh_up_w': _L0_ffn_in['sh_up_w'], 'L0_ffn_sh_down_w': _L0_ffn_in['sh_down_w']}
    _x0 = _d['L0_attn_x']
    _d['L0_attn_x'] = jax.random.normal(jax.random.fold_in(jax.random.key(seed), 1), (4, 1024, 256), dtype=_x0.dtype)
    del _x0
    return _d

def reference(L0_attn_x, L0_attn_in_proj_w, L0_attn_conv_w, L0_attn_conv_b, L0_attn_A_param, L0_attn_ln_w, L0_attn_ln_b, L0_attn_out_proj_w, L0_ffn_router_weight, L0_ffn_e_bias, L0_ffn_gate_w, L0_ffn_up_w, L0_ffn_down_w, L0_ffn_sh_gate_w, L0_ffn_sh_up_w, L0_ffn_sh_down_w):

    def _L0_attn_ref(x, in_proj_w, conv_w, conv_b, A_param, ln_w, ln_b, out_proj_w):
        import jax, jax.numpy as jnp
        import numpy as np
        D_MODEL = 256
        D_STATE = 64
        D_HEAD = 64
        N_HEADS = 16
        D_INNER = D_HEAD * N_HEADS
        K = 4
        BATCH = 4
        SEQ = 1024
        LN_EPS = 1e-05

        def _ssd_scan(xh, Bm, Cm, A_param):
            A_disc = jnp.exp(-jnp.exp(A_param))

            def step(h, inp):
                x_t, B_t, C_t = inp
                h = h * A_disc + B_t[:, None, None, :] * x_t[..., None]
                y_t = jnp.einsum('bhdn,bn->bhd', h, C_t)
                return (h, y_t)
            b = xh.shape[0]
            h0 = jnp.zeros((b, N_HEADS, D_HEAD, D_STATE), xh.dtype)
            xs = (jnp.swapaxes(xh, 0, 1), jnp.swapaxes(Bm, 0, 1), jnp.swapaxes(Cm, 0, 1))
            _, ys = jax.lax.scan(step, h0, xs)
            return jnp.swapaxes(ys, 0, 1)
        b, L, _ = x.shape
        xBC = x @ in_proj_w.T
        xc = xBC[..., :D_INNER]
        z = xBC[..., D_INNER:2 * D_INNER]
        Bm = xBC[..., 2 * D_INNER:2 * D_INNER + D_STATE]
        Cm = xBC[..., 2 * D_INNER + D_STATE:]
        xt = jnp.swapaxes(xc, 1, 2)
        y = jax.lax.conv_general_dilated(xt, conv_w, window_strides=(1,), padding=[(K - 1, 0)], feature_group_count=D_INNER, dimension_numbers=('NCH', 'OIH', 'NCH'))
        xc = jnp.swapaxes(y + conv_b[None, :, None], 1, 2)
        xc = jax.nn.silu(xc)
        xh = xc.reshape(b, L, N_HEADS, D_HEAD)
        yssd = _ssd_scan(xh, Bm, Cm, A_param).reshape(b, L, D_INNER)
        yg = yssd * jax.nn.silu(z)
        mu = yg.mean(-1, keepdims=True)
        var = yg.var(-1, keepdims=True)
        yn = (yg - mu) / jnp.sqrt(var + LN_EPS) * ln_w + ln_b
        return yn @ out_proj_w.T

    def _L0_ffn_ref(hidden_states, router_weight, e_bias, gate_w, up_w, down_w, sh_gate_w, sh_up_w, sh_down_w):
        import jax, jax.numpy as jnp
        import numpy as np
        B, S, H = (1, 512, 256)
        E, K = (16, 4)
        G, TG = (4, 2)
        I_MOE = 128
        N_SH = 2
        SCALE = 2.5

        def _mlp(x, gw, uw, dw):
            return jax.nn.silu(x @ gw.T) * (x @ uw.T) @ dw.T

        def _route(x2d, router_weight, e_bias):
            T = x2d.shape[0]
            scores = jax.nn.sigmoid(x2d @ router_weight.T)
            sc = scores + e_bias[None, :]
            group_scores = jnp.sum(jax.lax.top_k(sc.reshape(T, G, E // G), 2)[0], axis=-1)
            _, gidx = jax.lax.top_k(group_scores, TG)
            gmask = jnp.zeros((T, G), sc.dtype).at[jnp.arange(T)[:, None], gidx].set(1.0)
            smask = jnp.repeat(gmask, E // G, axis=1)
            masked = jnp.where(smask > 0, sc, 0.0)
            _, tidx = jax.lax.top_k(masked, K)
            tw = jnp.take_along_axis(scores, tidx, axis=1)
            tw = tw / (jnp.sum(tw, axis=-1, keepdims=True) + 1e-20)
            tw = tw * SCALE
            return (tidx, tw)

        def _moe_forward(hidden_states, router_weight, e_bias, gate_w, up_w, down_w, sh_gate_w, sh_up_w, sh_down_w):
            orig_shape = hidden_states.shape
            x = hidden_states.reshape(-1, H)
            T = x.shape[0]
            tidx, tw = _route(x, router_weight, e_bias)
            g = jnp.einsum('th,eih->tei', x, gate_w)
            u = jnp.einsum('th,eih->tei', x, up_w)
            h = jax.nn.silu(g) * u
            yo = jnp.einsum('tei,ehi->teh', h, down_w)
            combine = jnp.zeros((T, E), tw.dtype).at[jnp.arange(T)[:, None], tidx].add(tw)
            routed = jnp.einsum('te,teh->th', combine, yo)
            shared = _mlp(hidden_states.reshape(-1, H), sh_gate_w, sh_up_w, sh_down_w)
            return (routed + shared).reshape(orig_shape)
        return _moe_forward(hidden_states, router_weight, e_bias, gate_w, up_w, down_w, sh_gate_w, sh_up_w, sh_down_w)
    x = L0_attn_x
    x = x + 0.5 * _L0_ffn_ref(_layernorm(x, axis=-1), L0_ffn_router_weight, L0_ffn_e_bias, L0_ffn_gate_w, L0_ffn_up_w, L0_ffn_down_w, L0_ffn_sh_gate_w, L0_ffn_sh_up_w, L0_ffn_sh_down_w)
    x = x + _L0_attn_ref(_layernorm(x, axis=-1), L0_attn_in_proj_w, L0_attn_conv_w, L0_attn_conv_b, L0_attn_A_param, L0_attn_ln_w, L0_attn_ln_b, L0_attn_out_proj_w)
    x = x + 0.5 * _L0_ffn_ref(_layernorm(x, axis=-1), L0_ffn_router_weight, L0_ffn_e_bias, L0_ffn_gate_w, L0_ffn_up_w, L0_ffn_down_w, L0_ffn_sh_gate_w, L0_ffn_sh_up_w, L0_ffn_sh_down_w)
    return x

_drawn_inputs = setup_inputs


def setup_inputs(seed=0):
    import zlib

    import numpy as np

    out = dict(_drawn_inputs(seed))
    spreads = {'L0_attn_ln_w': (1.0, 0.2), 'L0_attn_ln_b': (0.0, 0.1), 'L0_ffn_e_bias': (0.0, 0.52)}
    factors = {'L0_ffn_router_weight': 8.0,
     'L0_ffn_gate_w': 4.041,
     'L0_ffn_up_w': 4.003,
     'L0_ffn_down_w': 4.011,
     'L0_ffn_sh_gate_w': 3.55,
     'L0_ffn_sh_up_w': 3.536,
     'L0_ffn_sh_down_w': 3.525}
    for name, (base, spread) in spreads.items():
        noise = np.random.default_rng([zlib.crc32(name.encode()), seed]).standard_normal(out[name].shape)
        drawn = base * np.exp(spread * noise) if base else spread * noise
        out[name] = jnp.asarray(drawn.astype(out[name].dtype))
    for name, factor in factors.items():
        out[name] = (out[name] * factor).astype(out[name].dtype)
    return out
```

```python
from contextlib import ExitStack

import concourse.bass as bass
from concourse import mybir

P = 128
D = 256
KT = D // P
TOK = 4096
TILE = 512
SUB = TILE // P
NT = TOK // TILE
E = 16
NU = E + 2
GROUPS = 4
EPG = E // GROUPS
HS = 3
RING = 4
SENTINEL = -3.0e38
TAKEN = -2.0e38
LN_EPS = 1e-5
DI = 1024
CT = DI // P
NST = 64
HALF = P // 2
TAPS = 4
BATCH = 4
PAIRS = DI // 2
COL_Z, COL_BC, COL_CB = DI, 2 * DI, 2 * DI + P
NCOL = 2 * DI + 2 * P
MAX_RATE = 1.25

F32 = mybir.dt.float32
F32R = mybir.dt.float32r
U32 = mybir.dt.uint32
I32 = mybir.dt.int32
ALU = mybir.AluOpType
ACT = mybir.ActivationFunctionType
AX = mybir.AxisListType



def ffn_block(nc, ctx, whole, consts, label, src, dst, gate_rows, w):
    ident = consts["ident"]

    def sb(name, shape, dt=F32):
        return ctx.enter_context(nc.sbuf_tensor(f"{label}_{name}", shape, dt))

    def psum(name, shape):
        return ctx.enter_context(nc.psum_tensor(f"{label}_{name}", shape, F32))

    def sem(name):
        return whole.enter_context(nc.semaphore(f"{label}_{name}"))

    gu_ps = psum("gu_ps", [P, 2, 2, TILE])
    acc_ps = psum("acc_ps", [P, KT, TILE])
    tr_ps = psum("tr_ps", [P, 2, TILE])

    wgu_hi = sb("wgu_hi", [P, NU, KT, 2, P], F32R)
    wgu_lo = sb("wgu_lo", [P, NU, KT, 2, P], F32R)
    wd_hi = sb("wd_hi", [P, NU, D], F32R)
    wd_lo = sb("wd_lo", [P, NU, D], F32R)
    wr_raw = sb("wr_raw", [P, KT, P])
    wr_hi = sb("wr_hi", [P, KT, P], F32R)
    wr_lo = sb("wr_lo", [P, KT, P], F32R)
    raw = sb("raw", [P, 4, 3 * D])
    bias = sb("bias", [P, E])
    later = sb("later", [P, GROUPS])
    half_neg = sb("half_neg", [P, SUB])
    x_ln = sb("x_ln", [P, SUB, D])
    x_res = sb("x_res", [P, SUB, D])
    xn = sb("xn", [P, SUB, D])
    bn = sb("bn", [P, SUB, 6])
    mv = sb("mv", [P, SUB, 2])
    var = sb("var", [P, SUB])
    rstd = sb("rstd", [P, SUB])
    xT_hi = sb("xT_hi", [P, 2, KT, TILE], F32R)
    xT_lo = sb("xT_lo", [P, 2, KT, TILE], F32R)
    scT = sb("scT", [P, TILE])
    score = sb("score", [P, SUB, E])
    sc = sb("sc", [P, SUB, E])
    pmax = sb("pmax", [P, SUB, GROUPS, 2])
    pmin = sb("pmin", [P, SUB, GROUPS, 2])
    top1 = sb("top1", [P, SUB, GROUPS])
    mid1 = sb("mid1", [P, SUB, GROUPS])
    mid2 = sb("mid2", [P, SUB, GROUPS])
    gsum = sb("gsum", [P, SUB, GROUPS])
    grank = sb("grank", [P, SUB, GROUPS])
    beats = sb("beats", [P, SUB, GROUPS])
    gmask = sb("gmask", [P, SUB, GROUPS], U32)
    seek = sb("seek", [P, SUB, E + 4])
    found = sb("found", [P, SUB, E + 4])
    top8 = sb("top8", [P, SUB, 8])
    picked = sb("picked", [P, SUB, E])
    tsum = sb("tsum", [P, SUB])
    trec = sb("trec", [P, SUB])
    comb = sb("comb", [P, SUB, 32])
    combT = sb("combT", [P, P])
    gate_b = sb("gate_b", [P, RING, TILE])
    sg = sb("sg", [P, 2, TILE])
    h = sb("h", [P, HS, TILE])
    h_hi = sb("h_hi", [P, HS, TILE], F32R)
    h_lo = sb("h_lo", [P, HS, TILE], F32R)
    oT = sb("oT", [P, KT, TILE])

    raw_in = [sem(f"raw_in{i}") for i in range(4)]
    small_in = sem("small_in")
    w_hi_ready = sem("w_hi_ready")
    w_lo_ready = sem("w_lo_ready")
    init_done = sem("init_done")
    x_in = sem("x_in")
    res_in = sem("res_in")
    ln_read = sem("ln_read")
    var_ready = sem("var_ready")
    rstd_ready = sem("rstd_ready")
    xn_ready = sem("xn_ready")
    xT_in_psum = sem("xT_in_psum")
    xT_hi_ready = sem("xT_hi_ready")
    xT_lo_ready = sem("xT_lo_ready")
    logits_ready = sem("logits_ready")
    scT_ready = sem("scT_ready")
    score_in_psum = sem("score_in_psum")
    comb_ready = sem("comb_ready")
    comb_in_psum = sem("comb_in_psum")
    combT_ready = sem("combT_ready")
    rows_out = sem("rows_out")
    gate_in = [sem(f"gate_in{i}") for i in range(RING)]
    gu_ready = sem("gu_ready")
    silu_done = sem("silu_done")
    gated = sem("gated")
    h_ready = sem("h_ready")
    h_hi_ready = sem("h_hi_ready")
    h_lo_ready = sem("h_lo_ready")
    down_done = sem("down_done")
    oT_ready = sem("oT_ready")
    out_in_psum = sem("out_in_psum")
    out_ready = sem("out_ready")
    stored = sem("stored")
    chain = sem("chain")

    src_v = src.rearrange("(s p) d -> p s d", p=P)
    dst_v = dst.rearrange("(s p) d -> p s d", p=P)
    rows_v = gate_rows.rearrange("(q m) t -> q m t", q=2)

    NI = 3

    def settle(eng):
        eng.wait_ge(init_done, NI)

    block = ctx.enter_context(nc.Block())

    @block.sync
    def _(sp):
        sp.dma_start(x_ln[:], src_v[:, 0:SUB, :]).then_inc(x_in, 16)
        sp.dma_start(bias[:], w["e_bias"].partition_broadcast(P)).then_inc(small_in, 16)
        sp.wait_ge(init_done, NI)
        sp.dma_start(wr_raw[:, :, 0:E], w["router"]).then_inc(small_in, 16)
        for n in range(NU):
            if n >= 4:
                sp.wait_ge(w_lo_ready, 1 + n - 3)
            sp.dma_start(raw[:, n % 4, 0:2 * D], w["gate_up"][:, n, :]).then_inc(raw_in[n % 4], 16)
            sp.dma_start(raw[:, n % 4, 2 * D:3 * D], w["down"][:, n, :]).then_inc(raw_in[n % 4], 16)

        def store_rows(t, par):
            if isinstance(t, int):
                sp.wait_ge(combT_ready, t + 1)
            else:
                settle(sp)
                sp.wait_ge(gated, E * (t - 1))
                sp.wait_ge(combT_ready, t + 1)
            sp.dma_start(rows_v[par], combT[:]).then_inc(rows_out, 16)

        store_rows(0, 0)
        with sp.Fori(0, NT // 2) as i:
            for par in range(2):
                t = i * 2 + par
                at, nxt = sp.snap(t * SUB), sp.snap(((t + 1) % NT) * SUB)
                stores, done = sp.snap(16 * (t + 1)), sp.snap(t + 1)
                for n in range(E):
                    if n == 0:
                        sp.wait_ge(rows_out, stores)
                        sp.wait_ge(ln_read, done)
                        sp.dma_start(x_ln[:], src_v[:, bass.ds(nxt, SUB), :]).then_inc(x_in, 16)
                    if n >= RING:
                        sp.wait_ge(gated, E * t + n - RING + 1)
                    row = rows_v[par].rearrange("(s e) t -> e s t", e=32)[n]
                    sp.dma_start(gate_b[:, n % RING, :].rearrange("p (s t) -> p s t", s=SUB),
                                 row.partition_broadcast(P)).then_inc(gate_in[n % RING], 16)
                    if n == 4:
                        sp.wait_ge(stored, 16 * t)
                        sp.dma_start(x_res[:], src_v[:, bass.ds(at, SUB), :]).then_inc(res_in, 16)
                store_rows(t + 1, 1 - par)
                sp.wait_ge(out_ready, t + 1)
                sp.dma_start(dst_v[:, bass.ds(at, SUB), :], x_res[:]).then_inc(stored, 16)
        sp.wait_ge(stored, 16 * NT)
        sp.wait_ge(rows_out, 16 * (NT + 1))
        sp.wait_ge(x_in, 16 * (NT + 1))

    @block.gpsimd
    def _(pool):
        nc.gpsimd.memset(wr_raw[:], 0.0).then_inc(init_done, 1)
        nc.gpsimd.memset(comb[:], 0.0).then_inc(init_done, 1)
        nc.gpsimd.memset(half_neg[:], -0.5).then_inc(init_done, 1)
        pool.wait_ge(init_done, NI)

        def rstd_of(t):
            pool.wait_ge(var_ready, t + 1)
            nc.gpsimd.tensor_tensor(rstd[:], var[:], half_neg[:], ALU.pow).then_inc(rstd_ready, 1)

        pool.wait_ge(w_hi_ready, 1)
        nc.gpsimd.tensor_tensor(wr_lo[:], wr_raw[:], wr_hi[:].bitcast(F32), ALU.subtract).then_inc(w_lo_ready, 1)
        rstd_of(0)
        for n in range(NU):
            pool.wait_ge(w_hi_ready, 1 + 2 * (n + 1))
            nc.gpsimd.tensor_tensor(wgu_lo[:, n].rearrange("p k g i -> p (k g i)"), raw[:, n % 4, 0:2 * D],
                                    wgu_hi[:, n].rearrange("p k g i -> p (k g i)").bitcast(F32), ALU.subtract)
            nc.gpsimd.tensor_tensor(wd_lo[:, n, :], raw[:, n % 4, 2 * D:3 * D], wd_hi[:, n, :].bitcast(F32),
                                    ALU.subtract).then_inc(w_lo_ready, 1)
        with pool.Fori(0, NT // 2) as i:
            for par in range(2):
                t = i * 2 + par
                for n in range(E):
                    pool.wait_ge(silu_done, NU * t + n + 1)
                    pool.wait_ge(gate_in[n % RING], 16 * (E // RING * t + n // RING + 1))
                    nc.gpsimd.tensor_tensor(sg[:, n % 2, :], sg[:, n % 2, :], gate_b[:, n % RING, :],
                                            ALU.mult).then_inc(gated, 1)
                    if n == 3:
                        rstd_of(t + 1)

    @block.scalar
    def _(act):
        act.wait_ge(small_in, 32)
        nc.scalar.copy(wr_hi[:], wr_raw[:]).then_inc(w_hi_ready, 1)

        def round_xT(t, par):
            act.wait_ge(xT_in_psum, t + 1)
            nc.scalar.copy(xT_hi[:, par], tr_ps[:]).then_inc(xT_hi_ready, 1)

        def squash(t):
            act.wait_ge(logits_ready, t + 1)
            nc.scalar.activation(scT[:], tr_ps[:, 0, :], ACT.Sigmoid).then_inc(scT_ready, 1)

        def copy_rows(t):
            act.wait_ge(comb_in_psum, t + 1)
            act.wait_ge(rows_out, 16 * t)
            nc.scalar.copy(combT[:], tr_ps[:, 0, 0:P]).then_inc(combT_ready, 1)

        def round_h(t, n):
            act.wait_ge(h_ready, NU * t + n + 3)
            act.wait_ge(down_done, NU * t + n + 1)
            nc.scalar.copy(h_hi[:, n % HS, :], h[:, n % HS, :]).then_inc(h_hi_ready, 1)

        round_xT(0, 0)
        squash(0)
        copy_rows(0)
        for n in range(NU):
            act.wait_ge(raw_in[n % 4], 32 * (n // 4 + 1))
            nc.scalar.copy(wgu_hi[:, n].rearrange("p k g i -> p (k g i)"), raw[:, n % 4, 0:2 * D]).then_inc(w_hi_ready, 1)
            nc.scalar.copy(wd_hi[:, n, :], raw[:, n % 4, 2 * D:3 * D]).then_inc(w_hi_ready, 1)
        with act.Fori(0, NT // 2) as i:
            for par in range(2):
                t = i * 2 + par
                for n in range(NU):
                    act.wait_ge(gu_ready, NU * t + n + 1)
                    nc.scalar.activation(sg[:, n % 2, :], gu_ps[:, n % 2, 0, :], ACT.Silu).then_inc(silu_done, 1)
                    if n >= 1:
                        round_h(t, n - 1)
                    if n == 6:
                        round_xT(t + 1, 1 - par)
                    if n == 9:
                        squash(t + 1)
                    if n == 14:
                        copy_rows(t + 1)
                round_h(t, NU - 1)
                act.wait_ge(down_done, NU * t + NU + HS)
                nc.scalar.mul(oT[:], acc_ps[:], 0.5).then_inc(oT_ready, 1)

    @block.vector
    def _(dve):
        links = [0]

        def link(ins):
            links[0] += 1
            ins.then_inc(chain, 1)
            dve.wait_ge(chain, links[0])

        def new_chain():
            dve.sem_clear(chain)
            links[0] = 0

        for g in range(GROUPS):
            link(nc.vector.memset(later[:, g:g + 1], float(GROUPS - 1 - g)))
        link(nc.vector.memset(seek[:], SENTINEL))
        nc.vector.memset(h[:, 0, 0:1], 0.0).then_inc(h_ready, 1)
        nc.vector.memset(h[:, 1, 0:1], 0.0).then_inc(h_ready, 1)
        dve.wait_ge(h_ready, 2)
        link(nc.vector.memset(h[:, 0, 0:1], 0.0))
        for s in range(HS):
            nc.vector.memset(top8[:, s, :], 0.0).then_inc(down_done, 1)
        dve.wait_ge(down_done, HS)

        def statistics(t):
            new_chain()
            dve.wait_ge(x_in, 16 * (t + 1))
            for s in range(SUB):
                link(nc.vector.bn_stats(bn[:, s, :], x_ln[:, s, :]))
            for s in range(SUB):
                link(nc.vector.bn_aggr(mv[:, s, :], bn[:, s, :]))
            nc.vector.tensor_scalar(var[:], mv[:, :, 1], LN_EPS, None, ALU.add).then_inc(var_ready, 1)

        def normalize(t):
            dve.wait_ge(rstd_ready, t + 1)
            if not isinstance(t, int):
                dve.wait_ge(xT_in_psum, t)
            for s in range(SUB):
                ins = nc.vector.tensor_scalar(xn[:, s, :], x_ln[:, s, :], mv[:, s, 0:1], rstd[:, s:s + 1],
                                              ALU.subtract, ALU.mult)
                ins.then_inc(xn_ready, 1)
                if s == SUB - 1:
                    dve.wait_ge(xn_ready, SUB * (t + 1))
            nc.vector.memset(bn[:, 0, 0:1], 0.0).then_inc(ln_read, 1)

        def rest_of_xT(t, par):
            dve.wait_ge(xT_hi_ready, t + 1)
            nc.vector.tensor_tensor(xT_lo[:, par], tr_ps[:], xT_hi[:, par].bitcast(F32),
                                    ALU.subtract).then_inc(xT_lo_ready, 1)

        def route(t):
            new_chain()
            dve.wait_ge(score_in_psum, t + 1)
            link(nc.vector.tensor_copy(score[:], tr_ps[:, 1, :].rearrange("p (s t) -> p s t", s=SUB)[:, :, 0:E]))
            link(nc.vector.tensor_tensor(sc[:], score[:], bias[:].unsqueeze(1).broadcast_to([P, SUB, E]), ALU.add))
            v = sc[:].rearrange("p s (g c) -> p s g c", c=EPG)
            link(nc.vector.tensor_tensor(pmax[:], v[:, :, :, 0:EPG:2], v[:, :, :, 1:EPG:2], ALU.max))
            link(nc.vector.tensor_tensor(pmin[:], v[:, :, :, 0:EPG:2], v[:, :, :, 1:EPG:2], ALU.min))
            link(nc.vector.tensor_tensor(top1[:], pmax[:, :, :, 0], pmax[:, :, :, 1], ALU.max))
            link(nc.vector.tensor_tensor(mid1[:], pmax[:, :, :, 0], pmax[:, :, :, 1], ALU.min))
            link(nc.vector.tensor_tensor(mid2[:], pmin[:, :, :, 0], pmin[:, :, :, 1], ALU.max))
            link(nc.vector.tensor_tensor(mid1[:], mid1[:], mid2[:], ALU.max))
            link(nc.vector.tensor_tensor(gsum[:], top1[:], mid1[:], ALU.add))
            link(nc.vector.tensor_copy(grank[:], later[:].unsqueeze(1).broadcast_to([P, SUB, GROUPS])))
            for d in range(1, GROUPS):
                m = GROUPS - d
                link(nc.vector.tensor_tensor(beats[:, :, 0:m], gsum[:, :, 0:m], gsum[:, :, d:], ALU.is_ge))
                link(nc.vector.tensor_tensor(grank[:, :, d:], grank[:, :, d:], beats[:, :, 0:m], ALU.add))
                link(nc.vector.tensor_tensor(grank[:, :, 0:m], grank[:, :, 0:m], beats[:, :, 0:m], ALU.subtract))
            link(nc.vector.tensor_scalar(gmask[:], grank[:], 2.0, None, ALU.is_lt))
            link(nc.vector.memset(seek[:, :, 0:E], 0.0))
            link(nc.vector.copy_predicated(seek[:, :, 0:E].rearrange("p s (g c) -> p s g c", c=EPG),
                                           gmask[:].unsqueeze(3).broadcast_to([P, SUB, GROUPS, EPG]), v))
            for s in range(SUB):
                link(nc.vector.max(top8[:, s, :], seek[:, s, :]))
            link(nc.vector.memset(top8[:, :, 4:8], SENTINEL))
            for s in range(SUB):
                link(nc.vector.match_replace(found[:, s, :], top8[:, s, :], seek[:, s, :], TAKEN))
            link(nc.vector.tensor_tensor(picked[:], found[:, :, 0:E], seek[:, :, 0:E], ALU.not_equal))
            link(nc.vector.tensor_tensor(picked[:], picked[:], score[:], ALU.mult))
            link(nc.vector.tensor_reduce(tsum[:], picked[:], AX.X, ALU.add))
            link(nc.vector.tensor_scalar(tsum[:], tsum[:], 1e-20, None, ALU.add))
            link(nc.vector.reciprocal(trec[:], tsum[:]))
            link(nc.vector.tensor_scalar(trec[:], trec[:], 2.5, None, ALU.mult))
            nc.vector.tensor_tensor(comb[:, :, 0:E], picked[:], trec[:].unsqueeze(2).broadcast_to([P, SUB, E]),
                                    ALU.mult).then_inc(comb_ready, 1)

        def gate(t, n):
            if n < E:
                dve.wait_ge(gated, E * t + n + 1)
            else:
                dve.wait_ge(silu_done, NU * t + n + 1)
            nc.vector.tensor_tensor(h[:, n % HS, :], gu_ps[:, n % 2, 1, :], sg[:, n % 2, :],
                                    ALU.mult).then_inc(h_ready, 1)

        def rest_of_h(t, n):
            dve.wait_ge(h_hi_ready, NU * t + n + 1)
            nc.vector.tensor_tensor(h_lo[:, n % HS, :], h[:, n % HS, :], h_hi[:, n % HS, :].bitcast(F32),
                                    ALU.subtract).then_inc(h_lo_ready, 1)

        dve.wait_ge(init_done, NI)
        statistics(0)
        normalize(0)
        rest_of_xT(0, 0)
        route(0)
        with dve.Fori(0, NT // 2) as i:
            for par in range(2):
                t = i * 2 + par
                for n in range(NU):
                    gate(t, n)
                    if n >= 1:
                        rest_of_h(t, n - 1)
                    if n == 1:
                        statistics(t + 1)
                    if n == 3:
                        normalize(t + 1)
                    if n == 6:
                        rest_of_xT(t + 1, 1 - par)
                    if n == 11:
                        route(t + 1)
                rest_of_h(t, NU - 1)
                dve.wait_ge(out_in_psum, t + 1)
                dve.wait_ge(res_in, 16 * (t + 1))
                nc.vector.tensor_tensor(x_res[:].rearrange("p s d -> p (s d)"), tr_ps[:].rearrange("p b t -> p (b t)"),
                                        x_res[:].rearrange("p s d -> p (s d)"), ALU.add).then_inc(out_ready, 1)

    @block.tensor
    def _(pe):
        def product(out, w_hi, w_lo, x_hi, x_lo, start, stop):
            nc.tensor.matmul(out, w_hi, x_hi, start=start, stop=False)
            nc.tensor.matmul(out, w_hi, x_lo, start=False, stop=False)
            return nc.tensor.matmul(out, w_lo, x_hi, start=False, stop=stop)

        def transpose_xn(t):
            pe.wait_ge(xn_ready, SUB * (t + 1))
            if not isinstance(t, int):
                pe.wait_ge(out_ready, t - 1)
            for k in range(KT):
                for s in range(SUB):
                    last = nc.tensor.transpose(tr_ps[:, k, s * P:(s + 1) * P], xn[:, s, k * P:(k + 1) * P], ident[:])
            last.then_inc(xT_in_psum, 1)

        def router(t, par):
            pe.wait_ge(xT_lo_ready, t + 1)
            for k in range(KT):
                last = product(tr_ps[:, 0, :], wr_hi[:, k, :], wr_lo[:, k, :], xT_hi[:, par, k, :], xT_lo[:, par, k, :],
                               k == 0, k == KT - 1)
            last.then_inc(logits_ready, 1)

        def transpose_scores(t):
            pe.wait_ge(scT_ready, t + 1)
            for s in range(SUB):
                last = nc.tensor.transpose(tr_ps[:, 1, s * P:(s + 1) * P], scT[:, s * P:(s + 1) * P], ident[:])
            last.then_inc(score_in_psum, 1)

        def transpose_comb(t):
            pe.wait_ge(comb_ready, t + 1)
            nc.tensor.transpose(tr_ps[:, 0, 0:P], comb[:].rearrange("p s e -> p (s e)"), ident[:]).then_inc(comb_in_psum, 1)

        def gate_up(t, par, n):
            pe.wait_ge(h_ready, NU * t + n + 1)
            pe.wait_ge(w_lo_ready, n + 2)
            for g in range(2):
                for k in range(KT):
                    last = product(gu_ps[:, n % 2, g, :], wgu_hi[:, n, k, g, :], wgu_lo[:, n, k, g, :],
                                   xT_hi[:, par, k, :], xT_lo[:, par, k, :], k == 0, k == KT - 1)
            last.then_inc(gu_ready, 1)

        def down(t, n):
            pe.wait_ge(h_lo_ready, NU * t + n + 1)
            if n == 0:
                pe.wait_ge(oT_ready, t)
            for k in range(KT):
                last = product(acc_ps[:, k, :], wd_hi[:, n, k * P:(k + 1) * P], wd_lo[:, n, k * P:(k + 1) * P],
                               h_hi[:, n % HS, :], h_lo[:, n % HS, :], n == 0, n == NU - 1)
            last.then_inc(down_done, 1)

        pe.wait_ge(consts["ident_ready"], consts["ident_count"])
        transpose_xn(0)
        pe.wait_ge(w_lo_ready, 1)
        router(0, 0)
        transpose_scores(0)
        transpose_comb(0)
        with pe.Fori(0, NT // 2) as i:
            for par in range(2):
                t = i * 2 + par
                for n in range(NU):
                    gate_up(t, par, n)
                    if n >= 2:
                        down(t, n - 2)
                    if n == 5:
                        transpose_xn(t + 1)
                    if n == 8:
                        router(t + 1, 1 - par)
                    if n == 10:
                        transpose_scores(t + 1)
                    if n == 13:
                        transpose_comb(t + 1)
                down(t, NU - 2)
                down(t, NU - 1)
                pe.wait_ge(oT_ready, t + 1)
                for s in range(SUB):
                    for k in range(KT):
                        col = s * D + k * P
                        last = nc.tensor.transpose(tr_ps[:, col // TILE, col % TILE:col % TILE + P],
                                                   oT[:, k, s * P:(s + 1) * P], ident[:])
                last.then_inc(out_in_psum, 1)


def attn_block(nc, ctx, whole, consts, label, src, dst, scratch, w):
    ident = consts["ident"]

    def sb(name, shape, dt=F32):
        return ctx.enter_context(nc.sbuf_tensor(f"{label}_{name}", shape, dt))

    def psum(name, shape):
        return ctx.enter_context(nc.psum_tensor(f"{label}_{name}", shape, F32))

    def sem(name):
        return whole.enter_context(nc.semaphore(f"{label}_{name}"))

    mm_ps = psum("mm_ps", [P, 2, TILE])
    xu_ps = psum("xu_ps", [P, 2, TILE])
    zy_ps = psum("zy_ps", [P, 2, TILE])
    y_ps = psum("y_ps", [P, 2, TILE])

    xs = sb("xs", [P, 2, CT, TILE])
    win_hi = sb("win_hi", [P, KT, NCOL], F32R)
    win_lo = sb("win_lo", [P, KT, NCOL], F32R)
    wout_hi = sb("wout_hi", [P, CT, D], F32R)
    wout_lo = sb("wout_lo", [P, CT, D], F32R)
    taps = sb("taps", [P, CT, TAPS])
    vecs = sb("vecs", [P, 3, CT])
    bias_out = sb("bias_out", [P, D])
    rate = sb("rate", [P, 1])
    expo = sb("expo", [P, 3, P])
    tab = sb("tab", [P, 3, P])
    chunk_decay = sb("chunk_decay", [P, 1])
    causal = sb("causal", [P, P], I32)
    ones = sb("ones", [P, P])
    flag_f = sb("flag_f", [P, 2])
    flag = sb("flag", [P, 1], I32)
    half_neg = sb("half_neg", [P, SUB])
    x_ln = sb("x_ln", [P, SUB, D])
    xn = sb("xn", [P, SUB, D])
    bn = sb("bn", [P, SUB, 6])
    mv = sb("mv", [P, SUB, 2])
    var = sb("var", [P, SUB])
    rstd = sb("rstd", [P, SUB])
    xT_hi = sb("xT_hi", [P, 2, KT, TILE], F32R)
    xT_lo = sb("xT_lo", [P, 2, KT, TILE], F32R)
    bc = sb("bc", [P, 2, TILE])
    g = sb("g", [P, 3, TILE])
    g1_hi = sb("g1_hi", [P, 2, TILE], F32R)
    g1_lo = sb("g1_lo", [P, 2, TILE], F32R)
    g23_hi = sb("g23_hi", [P, 2, TILE], F32R)
    g23_lo = sb("g23_lo", [P, 2, TILE], F32R)
    m_full = sb("m_full", [P, SUB, P])
    m_hi = sb("m_hi", [P, 2, SUB, P], F32R)
    m_lo = sb("m_lo", [P, 2, SUB, P], F32R)
    bo_hi = sb("bo_hi", [P, 2, SUB, P], F32R)
    bo_lo = sb("bo_lo", [P, 2, SUB, P], F32R)
    raw = sb("raw", [P, 2, TAPS - 1 + TILE])
    zeros = sb("zeros", [P, TAPS - 1])
    carry = sb("carry", [P, CT, TAPS - 1])
    X_hi = sb("X_hi", [P, DI], F32R)
    X_lo = sb("X_lo", [P, DI], F32R)
    S = sb("S", [P, DI])
    S_hi = sb("S_hi", [P, DI], F32R)
    S_lo = sb("S_lo", [P, DI], F32R)
    sz = sb("sz", [P, DI])
    yn = sb("yn", [P, DI])
    ybn = sb("ybn", [P, 2, 6])
    ymv = sb("ymv", [P, 2])
    yvar = sb("yvar", [P, 1])
    yrstd = sb("yrstd", [P, 1])
    ynT_hi = sb("ynT_hi", [P, CT, P], F32R)
    ynT_lo = sb("ynT_lo", [P, CT, P], F32R)
    x_res = sb("x_res", [P, SUB, D])
    ga = sb("ga", [P, PAIRS])
    gs = sb("gs", [P, PAIRS])
    gx, gb, gc, gh = (S[:, i * P:(i + 1) * P] for i in range(4))
    gbc = S[:, 4 * P:6 * P].rearrange("p (k t) -> p k t", k=2)
    pick = sb("pick", [P, 2])

    names = """rate_ready w_in0 w_in1 small_in rate_in a_in ga_in w_hi w_lo init_p init_v init_a x_in ln_read var_ready rstd_ready
        xn_ready xT_in_psum xT_hi_ready xT_lo_ready bc_in_psum bc_copied g_ready g_hi_ready g_lo_ready bo_in_psum
        bo_hi_ready bo_lo_ready m_in_psum m_masked m_hi_ready m_lo_ready xp_in_psum raw_ready tap0_ready conv_done
        xs_ready X_in_psum X_hi_ready X_lo_ready z_in_psum z_ready y_in_psum y_gated yvar_ready yrstd_ready yn_ready
        yn_in_psum ynT_hi_ready ynT_lo_ready out_in_psum out_added u_in_psum S_ready S_hi_ready S_lo_ready
        res_in res_biased stored chain pchain flag_sum flag_ready bias_in_psum
        gx_out gbc_out gbc_in gx_in gh_ready pair_done gchain""".split()
    s = {n: sem(n) for n in names}

    def settle(eng):
        eng.wait_ge(s["init_p"], INIT_P)

    src_v = src.rearrange("(s p) d -> p s d", p=P)
    dst_v = dst.rearrange("(s p) d -> p s d", p=P)
    stage = xs[:].rearrange("p a c t -> p a (c t)")
    xg = scratch["x_rows"]
    bcg = scratch["bc_rows"]

    WP = 2
    PIECES = [(0, 1152), (1152, 2304)]
    INIT_P = 15

    block = ctx.enter_context(nc.Block())

    @block.sync
    def _(sp):
        def load_x(t):
            if isinstance(t, int):
                if t:
                    sp.wait_ge(s["ln_read"], t)
                sp.dma_start(x_ln[:], src_v[:, t * SUB:(t + 1) * SUB, :]).then_inc(s["x_in"], 16)
            else:
                at = sp.snap((t % NT) * SUB)
                sp.wait_ge(s["ln_read"], t)
                sp.dma_start(x_ln[:], src_v[:, bass.ds(at, SUB), :]).then_inc(s["x_in"], 16)

        load_x(0)
        for n, (a, b) in enumerate(PIECES):
            sp.dma_start(stage[:, n, 0:KT * (b - a)].rearrange("p (k c) -> p k c", k=KT),
                         w["in_proj"][:, :, a:b]).then_inc(s[f"w_in{n}"], 16)
        sp.dma_start(rate[0:HALF, :], w["A"][0, :].rearrange("(n o) -> n o", o=1)).then_inc(s["rate_in"], 16)
        sp.dma_start(rate[HALF:P, :], w["A"][0, :].rearrange("(n o) -> n o", o=1)).then_inc(s["rate_in"], 16)
        sp.dma_start(taps[:], w["conv_w"]).then_inc(s["small_in"], 16)
        for i, name in enumerate(("conv_b", "ln_w", "ln_b")):
            sp.dma_start(vecs[:, i, :], w[name]).then_inc(s["small_in"], 16)
        sp.dma_start(ga[:], w["A_pairs"]).then_inc(s["ga_in"], 16)
        sp.dma_start(S[:, 0:CT * NST].rearrange("p (j n) -> p j n", n=NST),
                     w["A"].rearrange("(j p) n -> p j n", p=P)).then_inc(s["a_in"], 16)
        sp.dma_start(sz[:, 0:NST], w["A"][0, :].partition_broadcast(P)).then_inc(s["a_in"], 16)
        load_x(1)
        sp.wait_ge(s["w_lo"], 1)
        sp.dma_start(stage[:, 0, 0:CT * D].rearrange("p (c d) -> p c d", c=CT), w["out_proj"]).then_inc(s["w_in0"], 16)

        sp.wait_ge(s["flag_ready"], 1)
        general = sp.value_load(flag[0:1, 0:1], min_val=0, max_val=1)

        def keep_bc(t, par):
            settle(sp)
            with sp.If(general == 1):
                sp.wait_ge(s["bc_copied"], 2 * (t + 1))
                sp.dma_start(bcg[par], bc[:]).then_inc(s["gbc_out"], 16)

        keep_bc(0, 0)
        with sp.Fori(0, BATCH) as b:
            for par in range(2):
                t = b * 2 + par
                at = sp.snap(t * SUB)
                load_x(t + 2)
                sp.wait_ge(s["stored"], 16 * t)
                sp.dma_start(x_res[:], src_v[:, bass.ds(at, SUB), :]).then_inc(s["res_in"], 16)
                for q in range(SUB):
                    chunks = sp.snap(SUB * t + q + 1)
                    kept, sent = sp.snap(16 * (t + 1)), sp.snap(16 * (SUB * t + q + 1))
                    settle(sp)
                    with sp.If(general == 1):
                        settle(sp)
                        sp.wait_ge(s["z_ready"], chunks)
                        sp.dma_start(xg.rearrange("(j p) t -> p j t", p=P),
                                     xs[:, par, :, q * P:(q + 1) * P]).then_inc(s["gx_out"], 16)
                        sp.wait_ge(s["gbc_out"], kept)
                        sp.dma_start(gbc, bcg[par][:, :, q * P:(q + 1) * P]).then_inc(s["gbc_in"], 16)
                        with sp.Fori(0, PAIRS) as pair:
                            for c in range(2):
                                if c == 0:
                                    sp.wait_ge(s["gx_out"], sent)
                                sp.dma_start(gx[c * HALF:(c + 1) * HALF, :],
                                             xg[bass.ds(pair * 2 + c, 1), :].broadcast_to([HALF, P])).then_inc(s["gx_in"], 16)
                            sp.wait_ge(s["pair_done"], 1)
                            sp.sem_clear(s["pair_done"])
                    if q == 0:
                        keep_bc(t + 1, 1 - par)
                sp.wait_ge(s["out_added"], SUB * (t + 1))
                sp.dma_start(dst_v[:, bass.ds(at, SUB), :], x_res[:]).then_inc(s["stored"], 16)
        sp.wait_ge(s["stored"], 16 * NT)
        sp.wait_ge(s["x_in"], 16 * (NT + 2))

    @block.gpsimd
    def _(pool):
        links = [0]

        def link(ins):
            links[0] += 1
            ins.then_inc(s["pchain"], 1)
            pool.wait_ge(s["pchain"], links[0])

        def new_chain():
            pool.sem_clear(s["pchain"])
            links[0] = 0

        G = nc.gpsimd
        made = [0]

        def make(ins):
            made[0] += 1
            ins.then_inc(s["init_p"], 1)
            pool.wait_ge(s["init_p"], made[0])

        pool.wait_ge(consts["ident_ready"], consts["ident_count"])
        lo, hi = slice(0, HALF), slice(HALF, P)
        kw = dict(channel_multiplier=0, allow_small_or_imprecise_dtypes=True)
        make(G.iota(expo[lo, 0, 0:HALF], [[-1, HALF]], base=HALF // 2, **kw))
        make(G.memset(expo[lo, 0, HALF:P], 0.0))
        make(G.iota(expo[hi, 0, :], [[1, P]], base=1, **kw))
        make(G.iota(expo[lo, 1, :], [[0, 2], [1, HALF]], base=-(HALF // 2), **kw))
        make(G.iota(expo[hi, 1, :], [[-1, P]], base=P - 1, **kw))
        make(G.iota(expo[lo, 2, :], [[-1, P]], base=HALF + HALF // 2, **kw))
        make(G.memset(expo[hi, 2, :], 0.0))
        make(G.memset(half_neg[:], -0.5))
        make(G.memset(zeros[:], 0.0))
        make(G.memset(m_full[:], 0.0))
        make(G.memset(ones[:], 1.0))
        make(G.memset(causal[:], 1))
        make(G.affine_select(out=causal[:], in_=causal[:], compare_op=ALU.is_ge, fill=0, base=0, pattern=[[1, P]],
                             channel_multiplier=-1))
        make(G.affine_select(out=pick[:, 0:1], in_=ones[:, 0:1], compare_op=ALU.is_ge, fill=0.0, base=HALF - 1,
                             pattern=[[0, 1]], channel_multiplier=-1))
        make(G.affine_select(out=pick[:, 1:2], in_=ones[:, 0:1], compare_op=ALU.is_ge, fill=0.0, base=-HALF,
                             pattern=[[0, 1]], channel_multiplier=1))

        def rstd_of(t):
            pool.wait_ge(s["var_ready"], t + 1)
            G.tensor_tensor(rstd[:], var[:], half_neg[:], ALU.pow).then_inc(s["rstd_ready"], 1)

        def scale_bc(t, par):
            pool.wait_ge(s["bc_copied"], 2 * (t + 1))
            for i, k in ((0, 0), (1, 1), (2, 0)):
                n = HALF if i == 2 else P
                G.tensor_tensor(g[0:n, i, :].rearrange("p (q t) -> p q t", q=SUB),
                                bc[0:n, k, :].rearrange("p (q t) -> p q t", q=SUB),
                                tab[0:n, i, :].unsqueeze(1).broadcast_to([n, SUB, P]), ALU.mult).then_inc(s["g_ready"], 1)

        def rest_of_g(t, par):
            pool.wait_ge(s["g_hi_ready"], 3 * (t + 1))
            for i, (gh_, gl_, n) in enumerate(((g1_hi[:, par, :], g1_lo[:, par, :], P),
                                               (g23_hi[:, 0, :], g23_lo[:, 0, :], P),
                                               (g23_hi[:, 1, :], g23_lo[:, 1, :], HALF))):
                G.tensor_tensor(gl_[0:n], g[0:n, i, :], gh_[0:n].bitcast(F32), ALU.subtract).then_inc(s["g_lo_ready"], 1)

        def rest_of_m(t, par):
            pool.wait_ge(s["m_hi_ready"], t + 1)
            G.tensor_tensor(m_lo[:, par], m_full[:], m_hi[:, par].bitcast(F32), ALU.subtract).then_inc(s["m_lo_ready"], 1)

        def first_tap(t, par, j):
            new_chain()
            settle(pool)
            pool.wait_ge(s["raw_ready"], CT * t + j + 1)
            before = raw[:, j % 2, 0:TAPS - 1]
            end = raw[:, j % 2, TILE:TILE + TAPS - 1]
            if par == 0:
                link(G.tensor_tensor(carry[:, j, :], end, zeros[:], ALU.add))
                link(G.memset(before, 0.0))
            else:
                link(G.tensor_tensor(before, carry[:, j, :], zeros[:], ALU.add))
                link(G.tensor_copy(carry[:, j, :], end))
            G.tensor_scalar(xs[:, par, j, :], raw[:, j % 2, 0:TILE], taps[:, j, 0:1], vecs[:, 0, j:j + 1],
                            ALU.mult, ALU.add).then_inc(s["tap0_ready"], 1)

        pool.wait_ge(s["init_a"], 1)
        G.tensor_scalar(rate[:], rate[:], -1.0, -MAX_RATE, ALU.mult, ALU.max).then_inc(s["rate_ready"], 1)
        rstd_of(0)
        for n, (a, b) in enumerate(PIECES):
            pool.wait_ge(s["w_hi"], n + 1)
            G.tensor_tensor(win_lo[:, :, a:b], stage[:, n, 0:KT * (b - a)].rearrange("p (k c) -> p k c", k=KT),
                            win_hi[:, :, a:b].bitcast(F32), ALU.subtract).then_inc(s["w_lo"], 1)
        pool.wait_ge(s["w_hi"], len(PIECES) + 1)
        G.tensor_tensor(wout_lo[:], stage[:, 1, 0:CT * D].rearrange("p (c d) -> p c d", c=CT), wout_hi[:].bitcast(F32),
                        ALU.subtract).then_inc(s["w_lo"], 1)
        rstd_of(1)
        pool.wait_ge(s["init_a"], 4)
        pool.wait_ge(s["small_in"], 64)
        scale_bc(0, 0)
        rest_of_g(0, 0)
        rest_of_m(0, 0)
        for j in range(CT):
            first_tap(0, 0, j)
        pool.wait_ge(s["flag_ready"], 1)
        general = pool.value_load(flag[0:1, 0:1], min_val=0, max_val=1)
        with pool.Fori(0, BATCH) as b:
            for par in range(2):
                t, nx = b * 2 + par, 1 - par
                for q in range(SUB):
                    if q == 0:
                        scale_bc(t + 1, nx)
                        pool.wait_ge(s["res_in"], 16 * (t + 1))
                        G.tensor_tensor(x_res[:], x_res[:], bias_out[:].unsqueeze(1).broadcast_to([P, SUB, D]),
                                        ALU.add).then_inc(s["res_biased"], 1)
                    if q == 2:
                        rest_of_m(t + 1, nx)
                    for j in {0: (), 1: (1,), 2: (3,), 3: (5,)}[q]:
                        first_tap(t + 1, nx, j)
                    pool.wait_ge(s["yvar_ready"], SUB * t + q + 1)
                    G.tensor_tensor(yrstd[:], yvar[:], half_neg[:, 0:1], ALU.pow).then_inc(s["yrstd_ready"], 1)
                    with pool.If(general == 0):
                        pool.wait_ge(s["S_hi_ready"], SUB * t + q + 1)
                        G.tensor_tensor(S_lo[:], S[:], S_hi[:].bitcast(F32),
                                        ALU.subtract).then_inc(s["S_lo_ready"], 1)
                    if q == 0:
                        rest_of_g(t + 1, nx)
                    for j in {0: (0,), 1: (2,), 2: (4,), 3: (6, 7)}[q]:
                        first_tap(t + 1, nx, j)
                    if q == 3:
                        rstd_of(t + 2)

    @block.scalar
    def _(act):
        A = nc.scalar
        act.wait_ge(s["rate_in"], 32)
        A.activation(rate[:], rate[:], ACT.Exp).then_inc(s["init_a"], 1)
        act.wait_ge(s["rate_ready"], 1)
        act.wait_ge(s["init_p"], INIT_P)
        A.activation(tab[:], expo[:], ACT.Exp, scale=rate[:, 0:1]).then_inc(s["init_a"], 1)
        act.wait_ge(s["init_a"], 2)
        A.mul(tab[0:HALF, 0, HALF:P], ones[0:HALF, 0:HALF], 0.0).then_inc(s["init_a"], 1)
        A.activation(chunk_decay[:], rate[:], ACT.Exp, scale=float(P)).then_inc(s["init_a"], 1)
        act.wait_ge(s["ga_in"], 16)
        A.activation(ga[:], ga[:], ACT.Exp).then_inc(s["init_a"], 1)
        act.wait_ge(s["init_a"], 5)
        A.activation(ga[:], ga[:], ACT.Exp, scale=-1.0).then_inc(s["init_a"], 1)
        act.wait_ge(s["a_in"], 32)
        A.activation(sz[:, NST:2 * NST], sz[:, 0:NST], ACT.Exp).then_inc(s["init_a"], 1)
        for n, (a, b) in enumerate(PIECES):
            act.wait_ge(s[f"w_in{n}"], 16)
            A.copy(win_hi[:, :, a:b], stage[:, n, 0:KT * (b - a)].rearrange("p (k c) -> p k c", k=KT)).then_inc(s["w_hi"], 1)
        act.wait_ge(s["bias_in_psum"], 1)
        A.copy(bias_out[:], mm_ps[:, 0, 0:D]).then_inc(s["init_a"], 1)
        act.wait_ge(s["init_v"], 2)
        A.copy(wout_hi[:], stage[:, 1, 0:CT * D].rearrange("p (c d) -> p c d", c=CT)).then_inc(s["w_hi"], 1)

        def round_xT(t, par):
            act.wait_ge(s["xT_in_psum"], t + 1)
            A.copy(xT_hi[:, par], mm_ps[:]).then_inc(s["xT_hi_ready"], 1)

        def copy_bc(t, par, i):
            act.wait_ge(s["bc_in_psum"], 2 * t + i + 1)
            if not isinstance(t, int):
                act.wait_ge(s["g_ready"], 3 * t)
            A.copy(bc[:, i, :], mm_ps[:, i, :]).then_inc(s["bc_copied"], 1)

        def round_g(t, par):
            act.wait_ge(s["g_ready"], 3 * (t + 1))
            A.copy(g1_hi[:, par, :], g[:, 0, :]).then_inc(s["g_hi_ready"], 1)
            A.copy(g23_hi[:, 0, :], g[:, 1, :]).then_inc(s["g_hi_ready"], 1)
            A.copy(g23_hi[0:HALF, 1, :], g[0:HALF, 2, :]).then_inc(s["g_hi_ready"], 1)

        def round_bo(t, par):
            act.wait_ge(s["bo_in_psum"], t + 1)
            A.copy(bo_hi[:, par].rearrange("p q t -> p (q t)"), mm_ps[:, 0, :]).then_inc(s["bo_hi_ready"], 1)

        def round_m(t, par):
            act.wait_ge(s["m_masked"], t + 1)
            A.copy(m_hi[:, par], m_full[:]).then_inc(s["m_hi_ready"], 1)

        def copy_xp(t, j):
            act.wait_ge(s["xp_in_psum"], CT * t + j + 1)
            if j >= 2:
                act.wait_ge(s["conv_done"], CT * t + j - 1)
            elif not isinstance(t, int):
                act.wait_ge(s["conv_done"], CT * t + j - 1)
            A.copy(raw[:, j % 2, TAPS - 1:], mm_ps[:, j % 2, :]).then_inc(s["raw_ready"], 1)

        def silu_x(t, par, j):
            act.wait_ge(s["conv_done"], CT * t + j + 1)
            A.activation(xs[:, par, j, :], xs[:, par, j, :], ACT.Silu).then_inc(s["xs_ready"], 1)

        def round_ynT(c):
            act.wait_ge(s["yn_in_psum"], c + 1)
            act.wait_ge(s["out_in_psum"], c)
            A.copy(ynT_hi[:].rearrange("p c t -> p (c t)"), zy_ps[:].rearrange("p b t -> p (b t)")).then_inc(s["ynT_hi_ready"], 1)

        round_xT(0, 0)
        round_xT(1, 1)
        for i in range(2):
            copy_bc(0, 0, i)
        round_g(0, 0)
        round_bo(0, 0)
        round_m(0, 0)
        for j in range(CT):
            copy_xp(0, j)
            if j >= 1:
                silu_x(0, 0, j - 1)
        silu_x(0, 0, CT - 1)
        act.wait_ge(s["flag_ready"], 1)
        general = act.value_load(flag[0:1, 0:1], min_val=0, max_val=1)
        with act.Fori(0, BATCH) as b:
            for par in range(2):
                t, nx = b * 2 + par, 1 - par
                for q in range(SUB):
                    c = SUB * t + q
                    act.wait_ge(s["X_in_psum"], c + 1)
                    act.wait_ge(s["u_in_psum"], c)
                    A.copy(X_hi[:], xu_ps[:].rearrange("p b t -> p (b t)")).then_inc(s["X_hi_ready"], 1)
                    act.wait_ge(s["z_in_psum"], c + 1)
                    act.wait_ge(s["y_gated"], c)
                    A.activation(sz[:], zy_ps[:].rearrange("p b t -> p (b t)"), ACT.Silu).then_inc(s["z_ready"], 1)
                    if q == 0:
                        with act.If(general == 1):
                            settle(act)
                            act.wait_ge(s["gbc_out"], 16 * (t + 1))
                            copy_bc(t + 1, nx, 0)
                        with act.Else():
                            settle(act)
                            copy_bc(t + 1, nx, 0)
                        copy_bc(t + 1, nx, 1)
                    if q == 1:
                        silu_x(t + 1, nx, 0)
                        round_bo(t + 1, nx)
                        silu_x(t + 1, nx, 1)
                    if q == 2:
                        silu_x(t + 1, nx, 2)
                        copy_xp(t + 1, 4)
                    if q == 3:
                        silu_x(t + 1, nx, 4)
                        copy_xp(t + 1, 6)
                        silu_x(t + 1, nx, 5)
                        copy_xp(t + 1, 7)
                    if q >= 1:
                        round_ynT(c - 1)
                    with act.If(general == 0):
                        act.wait_ge(s["S_ready"], c + 1)
                        A.copy(S_hi[:], S[:]).then_inc(s["S_hi_ready"], 1)
                    if q == 0:
                        round_g(t + 1, nx)
                        copy_xp(t + 1, 0)
                        copy_xp(t + 1, 1)
                    if q == 1:
                        round_m(t + 1, nx)
                        copy_xp(t + 1, 2)
                        copy_xp(t + 1, 3)
                    if q == 2:
                        silu_x(t + 1, nx, 3)
                        copy_xp(t + 1, 5)
                    if q == 3:
                        silu_x(t + 1, nx, 6)
                        silu_x(t + 1, nx, 7)
                        round_xT(t + 2, par)
                round_ynT(SUB * t + SUB - 1)

    @block.vector
    def _(dve):
        V = nc.vector
        links = [0]

        def link(ins):
            links[0] += 1
            ins.then_inc(s["chain"], 1)
            dve.wait_ge(s["chain"], links[0])

        def new_chain():
            dve.sem_clear(s["chain"])
            links[0] = 0

        def statistics(t):
            new_chain()
            dve.wait_ge(s["x_in"], 16 * (t + 1))
            for i in range(SUB):
                link(V.bn_stats(bn[:, i, :], x_ln[:, i, :]))
            for i in range(SUB):
                link(V.bn_aggr(mv[:, i, :], bn[:, i, :]))
            V.tensor_scalar(var[:], mv[:, :, 1], LN_EPS, None, ALU.add).then_inc(s["var_ready"], 1)

        def normalize(t):
            dve.wait_ge(s["rstd_ready"], t + 1)
            if not isinstance(t, int) or t:
                dve.wait_ge(s["xT_in_psum"], t)
            for i in range(SUB):
                V.tensor_scalar(xn[:, i, :], x_ln[:, i, :], mv[:, i, 0:1], rstd[:, i:i + 1],
                                ALU.subtract, ALU.mult).then_inc(s["xn_ready"], 1)
            dve.wait_ge(s["xn_ready"], SUB * (t + 1))
            V.memset(bn[:, 0, 0:1], 0.0).then_inc(s["ln_read"], 1)

        def rest_of_xT(t, par):
            dve.wait_ge(s["xT_hi_ready"], t + 1)
            V.tensor_tensor(xT_lo[:, par], mm_ps[:], xT_hi[:, par].bitcast(F32), ALU.subtract).then_inc(s["xT_lo_ready"], 1)

        def rest_of_bo(t, par):
            dve.wait_ge(s["bo_hi_ready"], t + 1)
            V.tensor_tensor(bo_lo[:, par].rearrange("p q t -> p (q t)"), mm_ps[:, 0, :],
                            bo_hi[:, par].rearrange("p q t -> p (q t)").bitcast(F32), ALU.subtract).then_inc(s["bo_lo_ready"], 1)

        def mask_m(t, par):
            settle(dve)
            dve.wait_ge(s["m_in_psum"], t + 1)
            if not isinstance(t, int):
                dve.wait_ge(s["m_lo_ready"], t)
            V.copy_predicated(m_full[:], causal[:].unsqueeze(1).broadcast_to([P, SUB, P]),
                              mm_ps[:, 1, :].rearrange("p (q t) -> p q t", q=SUB)).then_inc(s["m_masked"], 1)

        def convolve(t, par, j):
            new_chain()
            dve.wait_ge(s["tap0_ready"], CT * t + j + 1)
            acc = xs[:, par, j, :]
            for k in range(1, TAPS):
                ins = V.scalar_tensor_tensor(out=acc, in0=raw[:, j % 2, k:k + TILE], scalar=taps[:, j, k:k + 1], in1=acc,
                                             op0=ALU.mult, op1=ALU.add)
                if k < TAPS - 1:
                    link(ins)
            ins.then_inc(s["conv_done"], 1)

        def rest_of_ynT(c):
            dve.wait_ge(s["ynT_hi_ready"], c + 1)
            V.tensor_tensor(ynT_lo[:].rearrange("p c t -> p (c t)"), zy_ps[:].rearrange("p b t -> p (b t)"),
                            ynT_hi[:].rearrange("p c t -> p (c t)").bitcast(F32), ALU.subtract).then_inc(s["ynT_lo_ready"], 1)

        def add_out(t, c, q):
            dve.wait_ge(s["out_in_psum"], c + 1)
            dve.wait_ge(s["res_biased"], t + 1)
            V.tensor_tensor(x_res[:, q, :], xu_ps[:, 0, 0:D], x_res[:, q, :], ALU.add).then_inc(s["out_added"], 1)

        dve.wait_ge(s["a_in"], 32)
        link(V.tensor_tensor(S[:, 0:CT * NST].rearrange("p (j n) -> p j n", n=NST),
                             S[:, 0:CT * NST].rearrange("p (j n) -> p j n", n=NST),
                             sz[:, 0:NST].unsqueeze(1).broadcast_to([P, CT, NST]), ALU.not_equal))
        link(V.tensor_reduce(flag_f[:, 0:1], S[:, 0:CT * NST], AX.X, ALU.max))
        dve.wait_ge(s["init_a"], 7)
        link(V.tensor_scalar(sz[:, NST:2 * NST], sz[:, NST:2 * NST], MAX_RATE, None, ALU.is_gt))
        link(V.tensor_reduce(flag_f[:, 1:2], sz[:, NST:2 * NST], AX.X, ALU.max))
        V.tensor_tensor(flag_f[:, 0:1], flag_f[:, 0:1], flag_f[:, 1:2], ALU.add).then_inc(s["init_v"], 1)
        dve.wait_ge(s["flag_sum"], 1)
        V.tensor_scalar(flag[:], mm_ps[:, 1, 0:1], 0.5, None, ALU.is_gt).then_inc(s["flag_ready"], 1)
        statistics(0)
        normalize(0)
        dve.wait_ge(s["w_in0"], 32)
        dve.wait_ge(s["small_in"], 64)
        dve.wait_ge(s["bias_in_psum"], 1)
        dve.wait_ge(s["w_lo"], 2)
        V.tensor_tensor(stage[:, 1, 0:CT * D].rearrange("p (c d) -> p c d", c=CT),
                        stage[:, 0, 0:CT * D].rearrange("p (c d) -> p c d", c=CT),
                        vecs[:, 1, :].unsqueeze(2).broadcast_to([P, CT, D]), ALU.mult).then_inc(s["init_v"], 1)
        rest_of_xT(0, 0)
        statistics(1)
        normalize(1)
        rest_of_xT(1, 1)
        rest_of_bo(0, 0)
        mask_m(0, 0)
        for j in range(CT):
            convolve(0, 0, j)
        dve.wait_ge(s["flag_ready"], 1)
        general = dve.value_load(flag[0:1, 0:1], min_val=0, max_val=1)
        with dve.Fori(0, BATCH) as b:
            for par in range(2):
                t, nx = b * 2 + par, 1 - par
                for q in range(SUB):
                    c = SUB * t + q
                    first = par == 0 and q == 0
                    dve.wait_ge(s["X_hi_ready"], c + 1)
                    V.tensor_tensor(X_lo[:], xu_ps[:].rearrange("p b t -> p (b t)"), X_hi[:].bitcast(F32),
                                    ALU.subtract).then_inc(s["X_lo_ready"], 1)
                    if q == 1:
                        convolve(t + 1, nx, 1)
                        rest_of_bo(t + 1, nx)
                        mask_m(t + 1, nx)
                    if q == 2:
                        convolve(t + 1, nx, 3)
                    if q == 3:
                        convolve(t + 1, nx, 5)
                        statistics(t + 2)

                    with dve.If(general == 1):
                        new_chain()
                        dve.wait_ge(s["gbc_in"], 16 * (c + 1))
                        link(V.tensor_copy(gb[0:HALF, :], gbc[0:HALF, 0, :]))
                        link(V.tensor_copy(gb[HALF:P, :], gbc[HALF:P, 1, :]))
                        link(V.tensor_copy(gc[0:HALF, :], gbc[0:HALF, 1, :]))
                        link(V.tensor_copy(gc[HALF:P, :], gbc[HALF:P, 0, :]))
                        if first:
                            link(V.memset(gs[:], 0.0))
                        with dve.Fori(0, PAIRS) as pair:
                            dve.sem_clear(s["gchain"])
                            dve.wait_ge(s["gx_in"], 32)
                            dve.sem_clear(s["gx_in"])
                            V.tensor_tensor(gx, gx, gb, ALU.mult).then_inc(s["gchain"], 1)
                            dve.wait_ge(s["gchain"], 1)
                            V.tensor_tensor_scan(gh, ga[:, bass.ds(pair, 1)].broadcast_to([P, P]), gx,
                                                 gs[:, bass.ds(pair, 1)], ALU.mult, ALU.add).then_inc(s["gchain"], 1)
                            dve.wait_ge(s["gchain"], 2)
                            V.tensor_copy(gs[:, bass.ds(pair, 1)], gh[:, P - 1:P]).then_inc(s["gchain"], 1)
                            dve.wait_ge(s["gchain"], 3)
                            V.tensor_tensor(gh, gh, gc, ALU.mult).then_inc(s["gh_ready"], 1)
                        V.memset(flag_f[:, 1:2], 0.0).then_inc(s["S_ready"], 1)
                        settle(dve)
                        dve.wait_ge(s["S_ready"], c + 1)

                    new_chain()
                    dve.wait_ge(s["y_in_psum"], c + 1)
                    dve.wait_ge(s["z_ready"], c + 1)
                    dve.wait_ge(s["yn_in_psum"], c)
                    V.tensor_tensor(yn[:], y_ps[:].rearrange("p b t -> p (b t)"), sz[:], ALU.mult).then_inc(s["y_gated"], 1)
                    dve.wait_ge(s["y_gated"], c + 1)
                    for i in range(2):
                        link(V.bn_stats(ybn[:, i, :], yn[:, i * TILE:(i + 1) * TILE]))
                    link(V.bn_aggr(ymv[:], ybn[:]))
                    V.tensor_scalar(yvar[:], ymv[:, 1:2], LN_EPS, None, ALU.add).then_inc(s["yvar_ready"], 1)
                    if q >= 1:
                        rest_of_ynT(c - 1)
                    dve.wait_ge(s["yrstd_ready"], c + 1)
                    V.tensor_scalar(yn[:], yn[:], ymv[:, 0:1], yrstd[:, 0:1], ALU.subtract, ALU.mult).then_inc(s["yn_ready"], 1)
                    if q >= 1:
                        add_out(t, c - 1, q - 1)
                    with dve.If(general == 0):
                        dve.wait_ge(s["u_in_psum"], c + 1)
                        dve.wait_ge(s["S_lo_ready"], c)
                        u = xu_ps[:].rearrange("p b t -> p (b t)")
                        if first:
                            V.tensor_copy(S[:], u).then_inc(s["S_ready"], 1)
                        else:
                            V.scalar_tensor_tensor(out=S[:], in0=S[:], scalar=chunk_decay[:, 0:1], in1=u,
                                                   op0=ALU.mult, op1=ALU.add).then_inc(s["S_ready"], 1)
                    for j in {0: (0,), 1: (2,), 2: (4,), 3: (6, 7)}[q]:
                        convolve(t + 1, nx, j)
                    if q == 3:
                        normalize(t + 2)
                        rest_of_xT(t + 2, par)
                c = SUB * t + SUB - 1
                rest_of_ynT(c)
                add_out(t, c, SUB - 1)

    @block.tensor
    def _(pe):
        def product(out, w_hi, w_lo, x_hi, x_lo, start, stop):
            nc.tensor.matmul(out, w_hi, x_hi, start=start, stop=False)
            nc.tensor.matmul(out, w_hi, x_lo, start=False, stop=False)
            return nc.tensor.matmul(out, w_lo, x_hi, start=False, stop=stop)

        def transpose_xn(t):
            pe.wait_ge(s["xn_ready"], SUB * (t + 1))
            if isinstance(t, int):
                if t:
                    pe.wait_ge(s["xT_lo_ready"], t)
            else:
                pe.wait_ge(s["raw_ready"], CT * t)
            for k in range(KT):
                for i in range(SUB):
                    last = nc.tensor.transpose(mm_ps[:, k, i * P:(i + 1) * P], xn[:, i, k * P:(k + 1) * P], ident[:])
            last.then_inc(s["xT_in_psum"], 1)

        def project(out, col, par):
            for k in range(KT):
                last = product(out, win_hi[:, k, col:col + P], win_lo[:, k, col:col + P], xT_hi[:, par, k, :],
                               xT_lo[:, par, k, :], k == 0, k == KT - 1)
            return last

        def project_bc(t, par):
            pe.wait_ge(s["xT_lo_ready"], 2 if isinstance(t, int) else t + 1)
            project(mm_ps[:, 0, :], COL_BC, par).then_inc(s["bc_in_psum"], 1)
            project(mm_ps[:, 1, :], COL_CB, par).then_inc(s["bc_in_psum"], 1)

        def project_x(t, par, j):
            if j < 2:
                if isinstance(t, int):
                    if j == 0:
                        pe.wait_ge(s["bo_lo_ready"], t + 1)
                    else:
                        pe.wait_ge(s["m_masked"], t + 1)
                else:
                    pe.wait_ge(s["bc_copied"], 2 * t + j + 1)
            elif j < 4:
                if j == 2:
                    pe.wait_ge(s["bo_lo_ready"], t + 1)
                else:
                    pe.wait_ge(s["m_masked"], t + 1)
                pe.wait_ge(s["raw_ready"], CT * t + j - 1)
            else:
                pe.wait_ge(s["raw_ready"], CT * t + j - 1)
            project(mm_ps[:, j % 2, :], j * P, par).then_inc(s["xp_in_psum"], 1)

        def decays(t, par):
            if isinstance(t, int):
                pe.wait_ge(s["bc_copied"], 2 * (t + 1))
            else:
                pe.wait_ge(s["raw_ready"], CT * t + 2)
            pe.wait_ge(s["g_lo_ready"], 3 * (t + 1))
            for q in range(SUB):
                last = nc.tensor.transpose(mm_ps[:, 0, q * P:(q + 1) * P], g[:, 1, q * P:(q + 1) * P], ident[:])
            last.then_inc(s["bo_in_psum"], 1)
            for q in range(SUB):
                a = q * P
                for blk in range(2):
                    b_hi = g1_hi[0:HALF, par, a:a + P] if blk == 0 else g23_hi[0:HALF, 1, a:a + P]
                    b_lo = g1_lo[0:HALF, par, a:a + P] if blk == 0 else g23_lo[0:HALF, 1, a:a + P]
                    t0 = a + blk * HALF
                    last = product(mm_ps[:, 1, t0:t0 + HALF], b_hi, b_lo, g23_hi[0:HALF, 0, t0:t0 + HALF],
                                   g23_lo[0:HALF, 0, t0:t0 + HALF], True, True)
            last.then_inc(s["m_in_psum"], 1)

        def finish(c):
            pe.wait_ge(s["yn_ready"], c + 1)
            for j in range(CT):
                last = nc.tensor.transpose(zy_ps[:, j // SUB, (j % SUB) * P:(j % SUB + 1) * P], yn[:, j * P:(j + 1) * P], ident[:])
            last.then_inc(s["yn_in_psum"], 1)
            pe.wait_ge(s["ynT_lo_ready"], c + 1)
            for j in range(CT):
                last = product(xu_ps[:, 0, 0:D], ynT_hi[:, j, :], ynT_lo[:, j, :], wout_hi[:, j, :], wout_lo[:, j, :],
                               j == 0, j == CT - 1)
            last.then_inc(s["out_in_psum"], 1)

        pe.wait_ge(consts["ident_ready"], consts["ident_count"])
        pe.wait_ge(s["init_v"], 1)
        pe.wait_ge(s["init_p"], INIT_P)
        nc.tensor.matmul(mm_ps[:, 1, 0:1], ones[:], flag_f[:, 0:1], start=True, stop=True).then_inc(s["flag_sum"], 1)
        pe.wait_ge(s["w_in0"], 32)
        pe.wait_ge(s["small_in"], 64)
        pe.wait_ge(s["flag_ready"], 1)
        for j in range(CT):
            last = nc.tensor.matmul(mm_ps[:, 0, 0:D], vecs[:, 2, j:j + 1].broadcast_to([P, P]),
                                    stage[:, 0, j * D:(j + 1) * D], start=(j == 0), stop=(j == CT - 1))
        last.then_inc(s["bias_in_psum"], 1)
        pe.wait_ge(s["init_a"], 8)
        transpose_xn(0)
        transpose_xn(1)
        pe.wait_ge(s["w_lo"], 3)
        project_bc(0, 0)
        decays(0, 0)
        for j in range(CT):
            project_x(0, 0, j)
        general = pe.value_load(flag[0:1, 0:1], min_val=0, max_val=1)
        with pe.Fori(0, BATCH) as b:
            for par in range(2):
                t, nx = b * 2 + par, 1 - par
                for q in range(SUB):
                    c = SUB * t + q
                    first = par == 0 and q == 0
                    if q == 0:
                        pe.wait_ge(s["xs_ready"], CT * (t + 1))
                    pe.wait_ge(s["out_added"], c - 1 if q else c)
                    pe.wait_ge(s["S_ready"], c)
                    for j in range(CT):
                        last = nc.tensor.transpose(xu_ps[:, j // SUB, (j % SUB) * P:(j % SUB + 1) * P],
                                                   xs[:, par, j, q * P:(q + 1) * P], ident[:])
                    last.then_inc(s["X_in_psum"], 1)
                    pe.wait_ge(s["ynT_lo_ready"], c - 1 if q else c)
                    for n in range(2):
                        for k in range(KT):
                            col = COL_Z + n * TILE
                            xh, xl = xT_hi[:, par, k, q * P:(q + 1) * P], xT_lo[:, par, k, q * P:(q + 1) * P]
                            last = product(zy_ps[:, n, :], xh, xl, win_hi[:, k, col:col + TILE], win_lo[:, k, col:col + TILE],
                                           k == 0, k == KT - 1)
                    last.then_inc(s["z_in_psum"], 1)
                    if q == 0:
                        project_bc(t + 1, nx)
                    if q == 1:
                        decays(t + 1, nx)
                    if q == 2:
                        project_x(t + 1, nx, 4)
                    if q == 3:
                        project_x(t + 1, nx, 6)
                        project_x(t + 1, nx, 7)
                    pe.wait_ge(s["X_lo_ready"], c + 1)
                    pe.wait_ge(s["y_gated"], c)
                    with pe.If(general == 1):
                        nc.tensor.matmul(y_ps[:, 0, 0:2], ones[:], pick[:], start=True, stop=True).then_inc(s["u_in_psum"], 1)
                        with pe.Fori(0, PAIRS) as pair:
                            pe.wait_ge(s["gh_ready"], 1)
                            pe.sem_clear(s["gh_ready"])
                            nc.tensor.matmul(y_ps[:].rearrange("p b t -> p (b t)")[:, bass.ds(pair * 2, 2)], gh, pick[:],
                                             start=True, stop=True).then_inc(s["pair_done"], 1)
                        nc.tensor.matmul(y_ps[:, 1, TILE - 2:TILE], gh, pick[:], start=True, stop=True).then_inc(s["y_in_psum"], 1)
                    with pe.Else():
                        if q == 0:
                            pe.wait_ge(s["m_lo_ready"], t + 1)
                            pe.wait_ge(s["bo_lo_ready"], t + 1)
                        if not first:
                            pe.wait_ge(s["S_lo_ready"], c)
                        for n in range(2):
                            cols = slice(n * TILE, (n + 1) * TILE)
                            last = product(y_ps[:, n, :], m_hi[:, par, q, :], m_lo[:, par, q, :], X_hi[:, cols], X_lo[:, cols],
                                           True, first)
                            if not first:
                                ca = slice(q * P, (q + 1) * P)
                                last = product(y_ps[:, n, :], g1_hi[HALF:P, par, ca], g1_lo[HALF:P, par, ca],
                                               S_hi[HALF:P, cols], S_lo[HALF:P, cols], False, True)
                        last.then_inc(s["y_in_psum"], 1)
                    if q >= 1:
                        pe.wait_ge(s["z_ready"], c + 1)
                        finish(c - 1)
                    with pe.If(general == 0):
                        if q >= 1:
                            pe.wait_ge(s["out_added"], c)
                        for n in range(2):
                            cols = slice(n * TILE, (n + 1) * TILE)
                            last = product(xu_ps[:, n, :], bo_hi[:, par, q, :], bo_lo[:, par, q, :], X_hi[:, cols], X_lo[:, cols],
                                           True, True)
                        last.then_inc(s["u_in_psum"], 1)
                    for j in {0: (0, 1), 1: (2, 3), 2: (5,), 3: ()}[q]:
                        project_x(t + 1, nx, j)
                    if q == 3:
                        transpose_xn(t + 2)
                pe.wait_ge(s["z_ready"], SUB * (t + 1))
                pe.wait_ge(s["S_ready"], SUB * (t + 1))
                finish(SUB * t + SUB - 1)


def program(nc, x, in_proj, out_proj, conv_w, conv_b, ln_w, ln_b, A, A_pairs, gate_up, down, router, e_bias, out):
    def scratch(name, shape):
        return nc.dram_tensor(name, shape, F32, kind="Internal").ap()

    x1, x2 = scratch("x1", [TOK, D]), scratch("x2", [TOK, D])
    ffn_w = dict(gate_up=gate_up, down=down, router=router, e_bias=e_bias)
    attn_w = dict(in_proj=in_proj, out_proj=out_proj, conv_w=conv_w, conv_b=conv_b, ln_w=ln_w, ln_b=ln_b, A=A,
                  A_pairs=A_pairs)
    with ExitStack() as whole:
        ident = whole.enter_context(nc.sbuf_tensor("ident", [P, P], F32))
        ident_ready = whole.enter_context(nc.semaphore("ident_ready"))
        nc.gpsimd.memset(ident[:], 0.0).then_inc(ident_ready, 1)
        nc.gpsimd.wait_ge(ident_ready, 1)
        nc.gpsimd.affine_select(out=ident[:], in_=ident[:], compare_op=ALU.not_equal, fill=1.0, base=0,
                                pattern=[[-1, P]], channel_multiplier=1).then_inc(ident_ready, 1)
        consts = dict(ident=ident, ident_ready=ident_ready, ident_count=2)
        with ExitStack() as ctx:
            ffn_block(nc, ctx, whole, consts, "f1", x, x1, scratch("rows1", [2 * P, P]), ffn_w)
        with ExitStack() as ctx:
            attn_block(nc, ctx, whole, consts, "at", x1, x2,
                       dict(x_rows=scratch("x_rows", [DI, P]), bc_rows=scratch("bc_rows", [2, P, 2, TILE])), attn_w)
        with ExitStack() as ctx:
            ffn_block(nc, ctx, whole, consts, "f2", x2, out, scratch("rows2", [2 * P, P]), ffn_w)


def kernel(**inputs):
    import numpy as np
    import concourse.bacc as bacc
    from concourse.bass_utils import run_bass_kernel_spmd

    i = {name: np.asarray(a) for name, a in inputs.items()}

    def channels(name):
        a = i[name].reshape(CT, P, -1).transpose(1, 0, 2)
        return a if a.shape[2] > 1 else a[:, :, 0]

    attn, ffn = "L0_attn_", "L0_ffn_"
    w_in = i[attn + "in_proj_w"]
    w_in = np.concatenate([w_in, w_in[COL_BC + NST:COL_BC + 2 * NST], w_in[COL_BC:COL_BC + NST]])
    halves = (NU - E, P, D)
    gate = np.concatenate([i[ffn + "gate_w"], i[ffn + "sh_gate_w"].reshape(halves)])
    up = np.concatenate([i[ffn + "up_w"], i[ffn + "sh_up_w"].reshape(halves)])
    down = np.concatenate([i[ffn + "down_w"], i[ffn + "sh_down_w"].reshape(D, 2, P).transpose(1, 0, 2)])
    arrays = dict(
        x=i[attn + "x"].reshape(TOK, D),
        in_proj=w_in.reshape(NCOL, KT, P).transpose(2, 1, 0),
        out_proj=i[attn + "out_proj_w"].reshape(D, CT, P).transpose(2, 1, 0),
        conv_w=channels(attn + "conv_w"),
        conv_b=channels(attn + "conv_b"),
        ln_w=channels(attn + "ln_w"),
        ln_b=channels(attn + "ln_b"),
        A=i[attn + "A_param"].reshape(DI, NST),
        A_pairs=i[attn + "A_param"].reshape(PAIRS, P).T,
        gate_up=np.stack([gate, up], 1).reshape(NU, 2, P, KT, P).transpose(4, 0, 3, 1, 2).reshape(P, NU, 2 * D),
        down=down.transpose(2, 0, 1),
        router=i[ffn + "router_weight"].reshape(E, KT, P).transpose(2, 1, 0),
        e_bias=i[ffn + "e_bias"],
    )
    nc = bacc.Bacc("TRN2", target_bir_lowering=False, num_devices=1)
    args, data = [], {}
    for name, a in arrays.items():
        data[f"in_{name}"] = np.ascontiguousarray(a)
        args.append(nc.dram_tensor(f"in_{name}", a.shape, mybir.dt.from_np(a.dtype), kind="ExternalInput").ap())
    args.append(nc.dram_tensor("out", (TOK, D), F32, kind="ExternalOutput").ap())
    program(nc, *args)
    result = run_bass_kernel_spmd(nc, [data], core_ids=[0])
    return result.results[0]["out"].reshape(i[attn + "x"].shape)
```

```python
from contextlib import ExitStack

import concourse.bass as bass
from concourse import mybir

P = 128
D = 256
KT = D // P
TOK = 4096
TILE = 512
SUB = TILE // P
NT = TOK // TILE
E = 16
SH = 2
NU = SH + E
GROUPS = 4
EPG = E // GROUPS
HS = 3
RING = 4
LAG = 2
AHEAD = 4
STORE_AT = 6
SENTINEL = -3.0e38
TAKEN = -2.0e38
LN_EPS = 1e-5
DI = 1024
CT = DI // P
NST = 64
HALF = P // 2
TAPS = 4
BATCH = 4
PAIRS = DI // 2
COL_Z, COL_BC, COL_CB = DI, 2 * DI, 2 * DI + P
NCOL = 2 * DI + 2 * P
MAX_RATE = 1.25

F32 = mybir.dt.float32
F32R = mybir.dt.float32r
U32 = mybir.dt.uint32
I32 = mybir.dt.int32
ALU = mybir.AluOpType
ACT = mybir.ActivationFunctionType
AX = mybir.AxisListType


def pairs_of_tiles(eng, body):
    for par in range(2):
        body(par, par)
    with eng.Fori(1, NT // 2) as i:
        for par in range(2):
            body(i * 2 + par, par)



def ffn_block(nc, ctx, whole, consts, label, src, dst, gate_rows, w):
    ident = consts["ident"]

    def sb(name, shape, dt=F32):
        return ctx.enter_context(nc.sbuf_tensor(f"{label}_{name}", shape, dt))

    def psum(name, shape):
        return ctx.enter_context(nc.psum_tensor(f"{label}_{name}", shape, F32))

    def sem(name):
        return whole.enter_context(nc.semaphore(f"{label}_{name}"))

    gu_ps = psum("gu_ps", [P, 2, 2, TILE])
    acc_ps = psum("acc_ps", [P, KT, TILE])
    tr_ps = psum("tr_ps", [P, 2, TILE])

    wgu_hi = sb("wgu_hi", [P, NU, KT, 2, P], F32R)
    wgu_lo = sb("wgu_lo", [P, NU, KT, 2, P], F32R)
    wd_hi = sb("wd_hi", [P, NU, D], F32R)
    wd_lo = sb("wd_lo", [P, NU, D], F32R)
    wr_raw = sb("wr_raw", [P, KT, P])
    wr_hi = sb("wr_hi", [P, KT, P], F32R)
    wr_lo = sb("wr_lo", [P, KT, P], F32R)
    raw = sb("raw", [P, 4, 3 * D])
    bias = sb("bias", [P, E])
    later = sb("later", [P, GROUPS])
    half_neg = sb("half_neg", [P, SUB])
    x_ln = sb("x_ln", [P, SUB, D])
    x_res = sb("x_res", [P, SUB, D])
    xn = sb("xn", [P, SUB, D])
    bn = sb("bn", [P, SUB, 6])
    mv = sb("mv", [P, SUB, 2])
    var = sb("var", [P, SUB])
    rstd = sb("rstd", [P, SUB])
    xT_hi = sb("xT_hi", [P, 2, KT, TILE], F32R)
    xT_lo = sb("xT_lo", [P, 2, KT, TILE], F32R)
    scT = sb("scT", [P, TILE])
    score = sb("score", [P, SUB, E])
    sc = sb("sc", [P, SUB, E])
    pmax = sb("pmax", [P, SUB, GROUPS, 2])
    pmin = sb("pmin", [P, SUB, GROUPS, 2])
    top1 = sb("top1", [P, SUB, GROUPS])
    mid1 = sb("mid1", [P, SUB, GROUPS])
    mid2 = sb("mid2", [P, SUB, GROUPS])
    gsum = sb("gsum", [P, SUB, GROUPS])
    grank = sb("grank", [P, SUB, GROUPS])
    beats = sb("beats", [P, SUB, GROUPS])
    gmask = sb("gmask", [P, SUB, GROUPS], U32)
    seek = sb("seek", [P, SUB, E + 4])
    found = sb("found", [P, SUB, E + 4])
    top8 = sb("top8", [P, SUB, 8])
    picked = sb("picked", [P, SUB, E])
    tsum = sb("tsum", [P, SUB])
    trec = sb("trec", [P, SUB])
    comb = sb("comb", [P, SUB, 32])
    combT = sb("combT", [P, P])
    gate_b = sb("gate_b", [P, RING, TILE])
    sg = sb("sg", [P, 2, TILE])
    h = sb("h", [P, HS, TILE])
    h_hi = sb("h_hi", [P, HS, TILE], F32R)
    h_lo = sb("h_lo", [P, HS, TILE], F32R)
    oT = sb("oT", [P, KT, TILE])

    raw_in = [sem(f"raw_in{i}") for i in range(4)]
    small_in = sem("small_in")
    w_hi_ready = sem("w_hi_ready")
    w_lo_ready = sem("w_lo_ready")
    init_done = sem("init_done")
    x_in = sem("x_in")
    res_in = sem("res_in")
    ln_read = sem("ln_read")
    var_ready = sem("var_ready")
    rstd_ready = sem("rstd_ready")
    xn_ready = sem("xn_ready")
    xT_in_psum = sem("xT_in_psum")
    xT_hi_ready = sem("xT_hi_ready")
    xT_lo_ready = sem("xT_lo_ready")
    logits_ready = sem("logits_ready")
    scT_ready = sem("scT_ready")
    score_in_psum = sem("score_in_psum")
    comb_ready = sem("comb_ready")
    comb_in_psum = sem("comb_in_psum")
    combT_ready = sem("combT_ready")
    rows_out = sem("rows_out")
    gate_in = [sem(f"gate_in{i}") for i in range(RING)]
    gu_ready = sem("gu_ready")
    silu_done = sem("silu_done")
    gated = sem("gated")
    h_ready = sem("h_ready")
    h_hi_ready = sem("h_hi_ready")
    h_lo_ready = sem("h_lo_ready")
    down_done = sem("down_done")
    oT_ready = sem("oT_ready")
    out_in_psum = sem("out_in_psum")
    out_ready = sem("out_ready")
    stored = sem("stored")
    chain = sem("chain")

    src_v = src.rearrange("(s p) d -> p s d", p=P)
    dst_v = dst.rearrange("(s p) d -> p s d", p=P)
    rows_v = gate_rows.rearrange("(q m) t -> q m t", q=2)

    NI = 3

    def after(eng, semaphore, count):
        if not isinstance(count, int) or count > 0:
            eng.wait_ge(semaphore, count)

    def settle(eng):
        eng.wait_ge(init_done, NI)

    block = ctx.enter_context(nc.Block())

    @block.sync
    def _(sp):
        sp.dma_start(x_ln[:], src_v[:, 0:SUB, :]).then_inc(x_in, 16)
        sp.dma_start(bias[:], w["e_bias"].partition_broadcast(P)).then_inc(small_in, 16)
        sp.wait_ge(init_done, NI)
        sp.dma_start(wr_raw[:, :, 0:E], w["router"]).then_inc(small_in, 16)
        def load_weights(n):
            if n >= 4:
                sp.wait_ge(w_lo_ready, 1 + n - 3)
            sp.dma_start(raw[:, n % 4, 0:2 * D], w["gate_up"][:, n, :]).then_inc(raw_in[n % 4], 16)
            sp.dma_start(raw[:, n % 4, 2 * D:3 * D], w["down"][:, n, :]).then_inc(raw_in[n % 4], 16)

        def load_x(t):
            if isinstance(t, int):
                sp.wait_ge(rows_out, 16 * t)
                sp.wait_ge(ln_read, t)
                sp.dma_start(x_ln[:], src_v[:, t * SUB:(t + 1) * SUB, :]).then_inc(x_in, 16)
            else:
                at, rows, done = sp.snap((t % NT) * SUB), sp.snap(16 * t), sp.snap(t)
                sp.wait_ge(rows_out, rows)
                sp.wait_ge(ln_read, done)
                sp.dma_start(x_ln[:], src_v[:, bass.ds(at, SUB), :]).then_inc(x_in, 16)

        def store_rows(t, par):
            if not isinstance(t, int):
                settle(sp)
            after(sp, gated, E * (t - 1))
            sp.wait_ge(combT_ready, t + 1)
            sp.dma_start(rows_v[par], combT[:]).then_inc(rows_out, 16)

        def load_gate(t, par, n):
            if not isinstance(t, int):
                settle(sp)
            after(sp, gated, E * t + n - RING + 1)
            row = rows_v[par].rearrange("(s e) t -> e s t", e=32)[n]
            sp.dma_start(gate_b[:, n % RING, :].rearrange("p (s t) -> p s t", s=SUB),
                         row.partition_broadcast(P)).then_inc(gate_in[n % RING], 16)

        def tile_of(v, t):
            if isinstance(t, int):
                return v[:, t * SUB:(t + 1) * SUB, :]
            return v[:, bass.ds(sp.snap(t * SUB), SUB), :]

        def store(t):
            settle(sp)
            to = tile_of(dst_v, t)
            sp.wait_ge(out_ready, t + 1)
            sp.dma_start(to, x_res[:]).then_inc(stored, 16)

        def load_res(t):
            settle(sp)
            of = tile_of(src_v, t)
            after(sp, stored, 16 * t)
            sp.dma_start(x_res[:], of).then_inc(res_in, 16)

        for n in range(AHEAD):
            load_weights(n)

        def tile(t, par):
            if isinstance(t, int) and t == 0:
                for n in range(SH):
                    load_weights(n + AHEAD)
                store_rows(0, 0)
            for n in range(E):
                if n == 0:
                    load_x(t + 1)
                load_gate(t, par, n)
                if isinstance(t, int) and t == 0 and SH + n + AHEAD < NU:
                    load_weights(SH + n + AHEAD)
                if n == STORE_AT and not (isinstance(t, int) and t == 0):
                    store(t - 1)
                if n == STORE_AT + 3:
                    load_res(t)
            store_rows(t + 1, 1 - par)

        pairs_of_tiles(sp, tile)
        store(NT - 1)
        sp.wait_ge(stored, 16 * NT)
        sp.wait_ge(rows_out, 16 * (NT + 1))
        sp.wait_ge(x_in, 16 * (NT + 1))

    @block.gpsimd
    def _(pool):
        nc.gpsimd.memset(wr_raw[:], 0.0).then_inc(init_done, 1)
        nc.gpsimd.memset(comb[:], 0.0).then_inc(init_done, 1)
        nc.gpsimd.memset(half_neg[:], -0.5).then_inc(init_done, 1)
        pool.wait_ge(init_done, NI)

        def rstd_of(t):
            pool.wait_ge(var_ready, t + 1)
            nc.gpsimd.tensor_tensor(rstd[:], var[:], half_neg[:], ALU.pow).then_inc(rstd_ready, 1)

        pool.wait_ge(w_hi_ready, 1)
        nc.gpsimd.tensor_tensor(wr_lo[:], wr_raw[:], wr_hi[:].bitcast(F32), ALU.subtract).then_inc(w_lo_ready, 1)
        rstd_of(0)

        def split_low(n):
            pool.wait_ge(w_hi_ready, 1 + 2 * (n + 1))
            nc.gpsimd.tensor_tensor(wgu_lo[:, n].rearrange("p k g i -> p (k g i)"), raw[:, n % 4, 0:2 * D],
                                    wgu_hi[:, n].rearrange("p k g i -> p (k g i)").bitcast(F32), ALU.subtract)
            nc.gpsimd.tensor_tensor(wd_lo[:, n, :], raw[:, n % 4, 2 * D:3 * D], wd_hi[:, n, :].bitcast(F32),
                                    ALU.subtract).then_inc(w_lo_ready, 1)

        for n in range(AHEAD):
            split_low(n)

        def tile(t, par):
            for n in range(NU):
                if n >= SH:
                    e = n - SH
                    pool.wait_ge(silu_done, NU * t + n + 1)
                    pool.wait_ge(gate_in[e % RING], 16 * (E // RING * t + e // RING + 1))
                    nc.gpsimd.tensor_tensor(sg[:, n % 2, :], sg[:, n % 2, :], gate_b[:, e % RING, :],
                                            ALU.mult).then_inc(gated, 1)
                if n == 2:
                    rstd_of(t + 1)

        pairs_of_tiles(pool, tile)

    @block.scalar
    def _(act):
        act.wait_ge(small_in, 32)
        nc.scalar.copy(wr_hi[:], wr_raw[:]).then_inc(w_hi_ready, 1)

        def round_xT(t, par):
            act.wait_ge(xT_in_psum, t + 1)
            nc.scalar.copy(xT_hi[:, par], tr_ps[:]).then_inc(xT_hi_ready, 1)

        def squash(t):
            act.wait_ge(logits_ready, t + 1)
            nc.scalar.activation(scT[:], tr_ps[:, 0, :], ACT.Sigmoid).then_inc(scT_ready, 1)

        def copy_rows(t):
            act.wait_ge(comb_in_psum, t + 1)
            after(act, rows_out, 16 * t)
            nc.scalar.copy(combT[:], tr_ps[:, 0, 0:P]).then_inc(combT_ready, 1)

        def round_h(t, n):
            act.wait_ge(h_ready, NU * t + n + 3)
            act.wait_ge(down_done, NU * t + n + 1)
            nc.scalar.copy(h_hi[:, n % HS, :], h[:, n % HS, :]).then_inc(h_hi_ready, 1)

        def split_high(n):
            act.wait_ge(raw_in[n % 4], 32 * (n // 4 + 1))
            nc.scalar.copy(wgu_hi[:, n].rearrange("p k g i -> p (k g i)"), raw[:, n % 4, 0:2 * D]).then_inc(w_hi_ready, 1)
            nc.scalar.copy(wd_hi[:, n, :], raw[:, n % 4, 2 * D:3 * D]).then_inc(w_hi_ready, 1)

        def take_sum(t):
            act.wait_ge(down_done, NU * (t + 1) + HS)
            nc.scalar.mul(oT[:], acc_ps[:], 0.5).then_inc(oT_ready, 1)

        split_high(0)
        split_high(1)
        round_xT(0, 0)
        squash(0)
        for n in range(2, AHEAD):
            split_high(n)

        def tile(t, par):
            first = isinstance(t, int) and t == 0
            for n in range(NU):
                act.wait_ge(gu_ready, NU * t + n + 1)
                nc.scalar.activation(sg[:, n % 2, :], gu_ps[:, n % 2, 0, :], ACT.Silu).then_inc(silu_done, 1)
                if n >= 1:
                    round_h(t, n - 1)
                elif not first:
                    round_h(t - 1, NU - 1)
                if n == 1 and not first:
                    take_sum(t - 1)
                if first and n + AHEAD < NU:
                    split_high(n + AHEAD)
                if first and n == 1:
                    copy_rows(0)
                if n == 7:
                    round_xT(t + 1, 1 - par)
                if n == 9:
                    squash(t + 1)
                if n == 16:
                    copy_rows(t + 1)

        pairs_of_tiles(act, tile)
        round_h(NT - 1, NU - 1)
        take_sum(NT - 1)

    @block.vector
    def _(dve):
        links = [0]

        def link(ins):
            links[0] += 1
            ins.then_inc(chain, 1)
            dve.wait_ge(chain, links[0])

        def new_chain():
            dve.sem_clear(chain)
            links[0] = 0

        def split_low(n):
            dve.wait_ge(w_hi_ready, 1 + 2 * (n + 1))
            dve.wait_ge(w_lo_ready, 1 + n)
            nc.vector.tensor_tensor(wgu_lo[:, n].rearrange("p k g i -> p (k g i)"), raw[:, n % 4, 0:2 * D],
                                    wgu_hi[:, n].rearrange("p k g i -> p (k g i)").bitcast(F32), ALU.subtract)
            nc.vector.tensor_tensor(wd_lo[:, n, :], raw[:, n % 4, 2 * D:3 * D], wd_hi[:, n, :].bitcast(F32),
                                    ALU.subtract).then_inc(w_lo_ready, 1)

        for g in range(GROUPS):
            link(nc.vector.memset(later[:, g:g + 1], float(GROUPS - 1 - g)))
        link(nc.vector.memset(seek[:], SENTINEL))
        nc.vector.memset(h[:, 0, 0:1], 0.0).then_inc(h_ready, 1)
        nc.vector.memset(h[:, 1, 0:1], 0.0).then_inc(h_ready, 1)
        dve.wait_ge(h_ready, 2)
        link(nc.vector.memset(h[:, 0, 0:1], 0.0))
        for s in range(HS):
            nc.vector.memset(top8[:, s, :], 0.0).then_inc(down_done, 1)
        dve.wait_ge(down_done, HS)

        def statistics(t):
            new_chain()
            dve.wait_ge(x_in, 16 * (t + 1))
            for s in range(SUB):
                link(nc.vector.bn_stats(bn[:, s, :], x_ln[:, s, :]))
            for s in range(SUB):
                link(nc.vector.bn_aggr(mv[:, s, :], bn[:, s, :]))
            nc.vector.tensor_scalar(var[:], mv[:, :, 1], LN_EPS, None, ALU.add).then_inc(var_ready, 1)

        def normalize(t):
            dve.wait_ge(rstd_ready, t + 1)
            after(dve, xT_in_psum, t)
            for s in range(SUB):
                ins = nc.vector.tensor_scalar(xn[:, s, :], x_ln[:, s, :], mv[:, s, 0:1], rstd[:, s:s + 1],
                                              ALU.subtract, ALU.mult)
                ins.then_inc(xn_ready, 1)
                if s == SUB - 1:
                    dve.wait_ge(xn_ready, SUB * (t + 1))
            nc.vector.memset(bn[:, 0, 0:1], 0.0).then_inc(ln_read, 1)

        def rest_of_xT(t, par):
            dve.wait_ge(xT_hi_ready, t + 1)
            nc.vector.tensor_tensor(xT_lo[:, par], tr_ps[:], xT_hi[:, par].bitcast(F32),
                                    ALU.subtract).then_inc(xT_lo_ready, 1)

        v = sc[:].rearrange("p s (g c) -> p s g c", c=EPG)

        def route_group_sums(t):
            new_chain()
            dve.wait_ge(score_in_psum, t + 1)
            link(nc.vector.tensor_copy(score[:], tr_ps[:, 1, :].rearrange("p (s t) -> p s t", s=SUB)[:, :, 0:E]))
            link(nc.vector.tensor_tensor(sc[:], score[:], bias[:].unsqueeze(1).broadcast_to([P, SUB, E]), ALU.add))
            link(nc.vector.tensor_tensor(pmax[:], v[:, :, :, 0:EPG:2], v[:, :, :, 1:EPG:2], ALU.max))
            link(nc.vector.tensor_tensor(pmin[:], v[:, :, :, 0:EPG:2], v[:, :, :, 1:EPG:2], ALU.min))
            link(nc.vector.tensor_tensor(top1[:], pmax[:, :, :, 0], pmax[:, :, :, 1], ALU.max))
            link(nc.vector.tensor_tensor(mid1[:], pmax[:, :, :, 0], pmax[:, :, :, 1], ALU.min))
            link(nc.vector.tensor_tensor(mid2[:], pmin[:, :, :, 0], pmin[:, :, :, 1], ALU.max))
            link(nc.vector.tensor_tensor(mid1[:], mid1[:], mid2[:], ALU.max))
            link(nc.vector.tensor_tensor(gsum[:], top1[:], mid1[:], ALU.add))

        def route_group_ranks():
            new_chain()
            link(nc.vector.tensor_copy(grank[:], later[:].unsqueeze(1).broadcast_to([P, SUB, GROUPS])))
            for d in range(1, GROUPS):
                m = GROUPS - d
                link(nc.vector.tensor_tensor(beats[:, :, 0:m], gsum[:, :, 0:m], gsum[:, :, d:], ALU.is_ge))
                link(nc.vector.tensor_tensor(grank[:, :, d:], grank[:, :, d:], beats[:, :, 0:m], ALU.add))
                link(nc.vector.tensor_tensor(grank[:, :, 0:m], grank[:, :, 0:m], beats[:, :, 0:m], ALU.subtract))

        def route_top_experts():
            new_chain()
            link(nc.vector.tensor_scalar(gmask[:], grank[:], 2.0, None, ALU.is_lt))
            link(nc.vector.memset(seek[:, :, 0:E], 0.0))
            link(nc.vector.copy_predicated(seek[:, :, 0:E].rearrange("p s (g c) -> p s g c", c=EPG),
                                           gmask[:].unsqueeze(3).broadcast_to([P, SUB, GROUPS, EPG]), v))
            for s in range(SUB):
                link(nc.vector.max(top8[:, s, :], seek[:, s, :]))
            link(nc.vector.memset(top8[:, :, 4:8], SENTINEL))
            for s in range(SUB):
                link(nc.vector.match_replace(found[:, s, :], top8[:, s, :], seek[:, s, :], TAKEN))

        def route_weights():
            new_chain()
            link(nc.vector.tensor_tensor(picked[:], found[:, :, 0:E], seek[:, :, 0:E], ALU.not_equal))
            link(nc.vector.tensor_tensor(picked[:], picked[:], score[:], ALU.mult))
            link(nc.vector.tensor_reduce(tsum[:], picked[:], AX.X, ALU.add))
            link(nc.vector.tensor_scalar(tsum[:], tsum[:], 1e-20, None, ALU.add))
            link(nc.vector.reciprocal(trec[:], tsum[:]))
            link(nc.vector.tensor_scalar(trec[:], trec[:], 2.5, None, ALU.mult))
            nc.vector.tensor_tensor(comb[:, :, 0:E], picked[:], trec[:].unsqueeze(2).broadcast_to([P, SUB, E]),
                                    ALU.mult).then_inc(comb_ready, 1)

        def gate(t, n):
            if n >= SH:
                dve.wait_ge(gated, E * t + n - SH + 1)
            else:
                dve.wait_ge(silu_done, NU * t + n + 1)
            nc.vector.tensor_tensor(h[:, n % HS, :], gu_ps[:, n % 2, 1, :], sg[:, n % 2, :],
                                    ALU.mult).then_inc(h_ready, 1)

        def rest_of_h(t, n):
            dve.wait_ge(h_hi_ready, NU * t + n + 1)
            nc.vector.tensor_tensor(h_lo[:, n % HS, :], h[:, n % HS, :], h_hi[:, n % HS, :].bitcast(F32),
                                    ALU.subtract).then_inc(h_lo_ready, 1)

        dve.wait_ge(init_done, NI)
        statistics(0)
        normalize(0)
        rest_of_xT(0, 0)
        route_group_sums(0)
        route_group_ranks()
        route_top_experts()
        route_weights()

        def add_residual(t):
            dve.wait_ge(out_in_psum, t + 1)
            dve.wait_ge(res_in, 16 * (t + 1))
            nc.vector.tensor_tensor(x_res[:].rearrange("p s d -> p (s d)"), tr_ps[:].rearrange("p b t -> p (b t)"),
                                    x_res[:].rearrange("p s d -> p (s d)"), ALU.add).then_inc(out_ready, 1)

        def tile(t, par):
            first = isinstance(t, int) and t == 0
            for n in range(NU):
                gate(t, n)
                if n >= 1:
                    rest_of_h(t, n - 1)
                elif not first:
                    rest_of_h(t - 1, NU - 1)
                if first and n + AHEAD < NU:
                    split_low(n + AHEAD)
                if n == 1:
                    statistics(t + 1)
                if n == 3 and not first:
                    add_residual(t - 1)
                if n == 4:
                    normalize(t + 1)
                if n == 7:
                    rest_of_xT(t + 1, 1 - par)
                if n == 11:
                    route_group_sums(t + 1)
                if n == 12:
                    route_group_ranks()
                if n == 13:
                    route_top_experts()
                if n == 14:
                    route_weights()

        pairs_of_tiles(dve, tile)
        rest_of_h(NT - 1, NU - 1)
        add_residual(NT - 1)

    @block.tensor
    def _(pe):
        def product(out, w_hi, w_lo, x_hi, x_lo, start, stop):
            nc.tensor.matmul(out, w_hi, x_hi, start=start, stop=False)
            nc.tensor.matmul(out, w_hi, x_lo, start=False, stop=False)
            return nc.tensor.matmul(out, w_lo, x_hi, start=False, stop=stop)

        def transpose_xn(t):
            pe.wait_ge(xn_ready, SUB * (t + 1))
            after(pe, out_ready, t - 1)
            for k in range(KT):
                for s in range(SUB):
                    last = nc.tensor.transpose(tr_ps[:, k, s * P:(s + 1) * P], xn[:, s, k * P:(k + 1) * P], ident[:])
            last.then_inc(xT_in_psum, 1)

        def router(t, par):
            pe.wait_ge(xT_lo_ready, t + 1)
            for k in range(KT):
                last = product(tr_ps[:, 0, :], wr_hi[:, k, :], wr_lo[:, k, :], xT_hi[:, par, k, :], xT_lo[:, par, k, :],
                               k == 0, k == KT - 1)
            last.then_inc(logits_ready, 1)

        def transpose_scores(t):
            pe.wait_ge(scT_ready, t + 1)
            for s in range(SUB):
                last = nc.tensor.transpose(tr_ps[:, 1, s * P:(s + 1) * P], scT[:, s * P:(s + 1) * P], ident[:])
            last.then_inc(score_in_psum, 1)

        def transpose_comb(t):
            pe.wait_ge(comb_ready, t + 1)
            nc.tensor.transpose(tr_ps[:, 0, 0:P], comb[:].rearrange("p s e -> p (s e)"), ident[:]).then_inc(comb_in_psum, 1)

        def gate_up(t, par, n):
            pe.wait_ge(h_ready, NU * t + n + 1)
            if isinstance(t, int) and t == 0:
                pe.wait_ge(w_lo_ready, n + 2)
            for g in range(2):
                for k in range(KT):
                    last = product(gu_ps[:, n % 2, g, :], wgu_hi[:, n, k, g, :], wgu_lo[:, n, k, g, :],
                                   xT_hi[:, par, k, :], xT_lo[:, par, k, :], k == 0, k == KT - 1)
            last.then_inc(gu_ready, 1)

        def down(t, n):
            pe.wait_ge(h_lo_ready, NU * t + n + 1)
            if n == 0:
                after(pe, oT_ready, t)
            for k in range(KT):
                last = product(acc_ps[:, k, :], wd_hi[:, n, k * P:(k + 1) * P], wd_lo[:, n, k * P:(k + 1) * P],
                               h_hi[:, n % HS, :], h_lo[:, n % HS, :], n == 0, n == NU - 1)
            last.then_inc(down_done, 1)

        def transpose_out(t):
            pe.wait_ge(oT_ready, t + 1)
            for s in range(SUB):
                for k in range(KT):
                    col = s * D + k * P
                    last = nc.tensor.transpose(tr_ps[:, col // TILE, col % TILE:col % TILE + P],
                                               oT[:, k, s * P:(s + 1) * P], ident[:])
            last.then_inc(out_in_psum, 1)

        def tile(t, par):
            first = isinstance(t, int) and t == 0
            for n in range(NU):
                gate_up(t, par, n)
                if first and n == 1:
                    transpose_comb(0)
                if n >= LAG:
                    down(t, n - LAG)
                elif not first:
                    down(t - 1, NU - LAG + n)
                if n == 2 and not first:
                    transpose_out(t - 1)
                if n == 6:
                    transpose_xn(t + 1)
                if n == 8:
                    router(t + 1, 1 - par)
                if n == 10:
                    transpose_scores(t + 1)
                if n == 16:
                    transpose_comb(t + 1)

        pe.wait_ge(consts["ident_ready"], consts["ident_count"])
        transpose_xn(0)
        pe.wait_ge(w_lo_ready, 1)
        router(0, 0)
        transpose_scores(0)
        pairs_of_tiles(pe, tile)
        for n in range(NU - LAG, NU):
            down(NT - 1, n)
        transpose_out(NT - 1)


def attn_block(nc, ctx, whole, consts, label, src, dst, scratch, w):
    ident = consts["ident"]

    def sb(name, shape, dt=F32):
        return ctx.enter_context(nc.sbuf_tensor(f"{label}_{name}", shape, dt))

    def psum(name, shape):
        return ctx.enter_context(nc.psum_tensor(f"{label}_{name}", shape, F32))

    def sem(name):
        return whole.enter_context(nc.semaphore(f"{label}_{name}"))

    mm_ps = psum("mm_ps", [P, 2, TILE])
    xu_ps = psum("xu_ps", [P, 2, TILE])
    zy_ps = psum("zy_ps", [P, 2, TILE])
    y_ps = psum("y_ps", [P, 2, TILE])

    xs = sb("xs", [P, 2, CT, TILE])
    win_hi = sb("win_hi", [P, KT, NCOL], F32R)
    win_lo = sb("win_lo", [P, KT, NCOL], F32R)
    wout = sb("wout", [P, CT, 2, D], F32R)
    taps = sb("taps", [P, CT, TAPS])
    vecs = sb("vecs", [P, 3, CT])
    bias_out = sb("bias_out", [P, D])
    rate = sb("rate", [P, 1])
    tab = sb("tab", [P, 3, P])
    chunk_decay = sb("chunk_decay", [P, 1])
    causal = sb("causal", [P, P], I32)
    flag_f = sb("flag_f", [P, 2])
    flag = sb("flag", [P, 1], I32)
    half_neg = sb("half_neg", [P, SUB])
    x_ln = sb("x_ln", [P, SUB, D])
    xn = sb("xn", [P, SUB, D])
    bn = sb("bn", [P, SUB, 6])
    mv = sb("mv", [P, SUB, 2])
    var = sb("var", [P, SUB])
    rstd = sb("rstd", [P, SUB])
    xT_hi = sb("xT_hi", [P, 2, KT, TILE], F32R)
    xT_lo = sb("xT_lo", [P, 2, KT, TILE], F32R)
    bc = sb("bc", [P, 2, TILE])
    g = sb("g", [P, 3, TILE])
    g1_hi = sb("g1_hi", [P, 2, TILE], F32R)
    g1_lo = sb("g1_lo", [P, 2, TILE], F32R)
    g23_hi = sb("g23_hi", [P, 2, TILE], F32R)
    g23_lo = sb("g23_lo", [P, 2, TILE], F32R)
    m_full = sb("m_full", [P, SUB, P])
    m_hi = sb("m_hi", [P, 2, SUB, P], F32R)
    m_lo = sb("m_lo", [P, 2, SUB, P], F32R)
    bo_hi = sb("bo_hi", [P, 2, SUB, P], F32R)
    bo_lo = sb("bo_lo", [P, 2, SUB, P], F32R)
    raw = sb("raw", [P, 2, TAPS - 1 + TILE])
    zeros = sb("zeros", [P, TAPS - 1])
    expo = raw[:].rearrange("p a t -> p (a t)")[:, 0:3 * P].rearrange("p (i t) -> p i t", i=3)
    ones = raw[:].rearrange("p a t -> p (a t)")[:, 3 * P:4 * P]
    tap0 = sb("tap0", [P, TILE])
    carry = sb("carry", [P, CT, TAPS - 1])
    X_hi = sb("X_hi", [P, DI], F32R)
    X_lo = sb("X_lo", [P, DI], F32R)
    S = sb("S", [P, DI])
    S_hi = sb("S_hi", [P, DI], F32R)
    S_lo = sb("S_lo", [P, DI], F32R)
    sz = sb("sz", [P, DI])
    yn = sb("yn", [P, DI])
    ybn = sb("ybn", [P, 2, 6])
    ymv = sb("ymv", [P, 2])
    yvar = sb("yvar", [P, 1])
    yrstd = sb("yrstd", [P, 1])
    ynT_hi = sb("ynT_hi", [P, CT, P], F32R)
    ynT_lo = sb("ynT_lo", [P, CT, P], F32R)
    x_res = sb("x_res", [P, SUB, D])
    ga = sb("ga", [P, PAIRS])
    gs = sb("gs", [P, PAIRS])
    gx, gb, gc, gh = (S[:, i * P:(i + 1) * P] for i in range(4))
    gbc = S[:, 4 * P:6 * P].rearrange("p (k t) -> p k t", k=2)
    pick = sb("pick", [P, 2])

    names = """rate_ready w_in0 w_in1 small_in rate_in a_in ga_in w_out w_hi w_lo w_lo_v init_p init_v init_a x_in ln_read var_ready rstd_ready
        xn_ready xT_in_psum xT_hi_ready xT_lo_ready bc_in_psum bc_copied g_ready g_hi_ready g_lo_ready bo_in_psum
        bo_hi_ready bo_lo_ready m_in_psum m_masked m_hi_ready m_lo_ready xp_in_psum raw_ready tap0_ready conv_done
        xs_ready X_in_psum X_hi_ready X_lo_ready z_in_psum z_ready y_in_psum y_gated yvar_ready yrstd_ready yn_ready
        yn_in_psum ynT_hi_ready ynT_lo_ready out_in_psum half_added out_added u_in_psum S_ready S_hi_ready S_lo_ready
        res_in res_biased stored chain pchain flag_sum flag_ready bias_in_psum
        gx_out gbc_out gbc_in gx_in gh_ready pair_done gchain""".split()
    s = {n: sem(n) for n in names}

    def after(eng, name, count):
        if not isinstance(count, int) or count > 0:
            eng.wait_ge(s[name], count)

    def settle(eng):
        eng.wait_ge(s["init_p"], INIT_P)

    src_v = src.rearrange("(s p) d -> p s d", p=P)
    dst_v = dst.rearrange("(s p) d -> p s d", p=P)
    HALF_COL = NCOL // 2
    PIECES = [(HALF_COL, NCOL), (0, HALF_COL)]
    stage = xs[:].rearrange("p a c t -> p (a c t)")
    win_raw = [stage[:, n * KT * HALF_COL:(n + 1) * KT * HALF_COL].rearrange("p (k c) -> p k c", k=KT) for n in range(2)]
    wout_raw = stage[:, KT * NCOL:KT * NCOL + CT * D].rearrange("p (c d) -> p c d", c=CT)
    xg = scratch["x_rows"]
    bcg = scratch["bc_rows"]

    INIT_P = 15

    block = ctx.enter_context(nc.Block())

    @block.sync
    def _(sp):
        def load_x(t):
            if isinstance(t, int):
                if t:
                    sp.wait_ge(s["ln_read"], t)
                sp.dma_start(x_ln[:], src_v[:, t * SUB:(t + 1) * SUB, :]).then_inc(s["x_in"], 16)
            else:
                at = sp.snap((t % NT) * SUB)
                sp.wait_ge(s["ln_read"], t)
                sp.dma_start(x_ln[:], src_v[:, bass.ds(at, SUB), :]).then_inc(s["x_in"], 16)

        load_x(0)
        sp.dma_start(rate[0:HALF, :], w["A"][0, :].rearrange("(n o) -> n o", o=1)).then_inc(s["rate_in"], 16)
        sp.dma_start(rate[HALF:P, :], w["A"][0, :].rearrange("(n o) -> n o", o=1)).then_inc(s["rate_in"], 16)
        sp.dma_start(taps[:], w["conv_w"]).then_inc(s["small_in"], 16)
        for i, name in enumerate(("conv_b", "ln_w", "ln_b")):
            sp.dma_start(vecs[:, i, :], w[name]).then_inc(s["small_in"], 16)
        sp.dma_start(ga[:], w["A_pairs"]).then_inc(s["ga_in"], 16)
        sp.dma_start(S[:, 0:CT * NST].rearrange("p (j n) -> p j n", n=NST),
                     w["A"].rearrange("(j p) n -> p j n", p=P)).then_inc(s["a_in"], 16)
        sp.dma_start(sz[:, 0:NST], w["A"][0, :].partition_broadcast(P)).then_inc(s["a_in"], 16)
        for n, (a, b) in enumerate(PIECES):
            sp.dma_start(win_raw[n], w["in_proj"][:, :, a:b]).then_inc(s[f"w_in{n}"], 16)
        sp.dma_start(wout_raw, w["out_proj"]).then_inc(s["w_out"], 16)
        load_x(1)

        sp.wait_ge(s["flag_ready"], 1)
        general = sp.value_load(flag[0:1, 0:1], min_val=0, max_val=1)

        def tile_of(v, t):
            if isinstance(t, int):
                return v[:, t * SUB:(t + 1) * SUB, :]
            return v[:, bass.ds(sp.snap(t * SUB), SUB), :]

        def keep_bc(t, par):
            settle(sp)
            with sp.If(general == 1):
                sp.wait_ge(s["bc_copied"], 2 * (t + 1))
                sp.dma_start(bcg[par], bc[:]).then_inc(s["gbc_out"], 16)

        keep_bc(0, 0)

        def store(t):
            settle(sp)
            to = tile_of(dst_v, t)
            sp.wait_ge(s["out_added"], SUB * (t + 1))
            sp.dma_start(to, x_res[:]).then_inc(s["stored"], 16)

        def load_res(t):
            settle(sp)
            of = tile_of(src_v, t)
            after(sp, "stored", 16 * t)
            sp.dma_start(x_res[:], of).then_inc(s["res_in"], 16)

        def tile(t, par):
            load_x(t + 2)
            for q in range(SUB):
                if isinstance(t, int):
                    chunks, kept, sent = SUB * t + q + 1, 16 * (t + 1), 16 * (SUB * t + q + 1)
                else:
                    chunks = sp.snap(SUB * t + q + 1)
                    kept, sent = sp.snap(16 * (t + 1)), sp.snap(16 * (SUB * t + q + 1))
                settle(sp)
                with sp.If(general == 1):
                    settle(sp)
                    sp.wait_ge(s["z_ready"], chunks)
                    sp.dma_start(xg.rearrange("(j p) t -> p j t", p=P),
                                 xs[:, par, :, q * P:(q + 1) * P]).then_inc(s["gx_out"], 16)
                    sp.wait_ge(s["gbc_out"], kept)
                    sp.dma_start(gbc, bcg[par][:, :, q * P:(q + 1) * P]).then_inc(s["gbc_in"], 16)
                    with sp.Fori(0, PAIRS) as pair:
                        for c in range(2):
                            if c == 0:
                                sp.wait_ge(s["gx_out"], sent)
                            sp.dma_start(gx[c * HALF:(c + 1) * HALF, :],
                                         xg[bass.ds(pair * 2 + c, 1), :].broadcast_to([HALF, P])).then_inc(s["gx_in"], 16)
                        sp.wait_ge(s["pair_done"], 1)
                        sp.sem_clear(s["pair_done"])
                if q == 0:
                    if not (isinstance(t, int) and t == 0):
                        store(t - 1)
                    load_res(t)
                if q == 1:
                    keep_bc(t + 1, 1 - par)

        pairs_of_tiles(sp, tile)
        store(NT - 1)
        sp.wait_ge(s["stored"], 16 * NT)
        sp.wait_ge(s["x_in"], 16 * (NT + 2))

    @block.gpsimd
    def _(pool):
        links = [0]

        def link(ins):
            links[0] += 1
            ins.then_inc(s["pchain"], 1)
            pool.wait_ge(s["pchain"], links[0])

        def new_chain():
            pool.sem_clear(s["pchain"])
            links[0] = 0

        G = nc.gpsimd
        made = [0]

        def make(ins):
            made[0] += 1
            ins.then_inc(s["init_p"], 1)
            pool.wait_ge(s["init_p"], made[0])

        pool.wait_ge(consts["ident_ready"], consts["ident_count"])
        lo, hi = slice(0, HALF), slice(HALF, P)
        kw = dict(channel_multiplier=0, allow_small_or_imprecise_dtypes=True)
        make(G.iota(expo[lo, 0, 0:HALF], [[-1, HALF]], base=HALF // 2, **kw))
        make(G.memset(expo[lo, 0, HALF:P], 0.0))
        make(G.iota(expo[hi, 0, :], [[1, P]], base=1, **kw))
        make(G.iota(expo[lo, 1, :], [[0, 2], [1, HALF]], base=-(HALF // 2), **kw))
        make(G.iota(expo[hi, 1, :], [[-1, P]], base=P - 1, **kw))
        make(G.iota(expo[lo, 2, :], [[-1, P]], base=HALF + HALF // 2, **kw))
        make(G.memset(expo[hi, 2, :], 0.0))
        make(G.memset(half_neg[:], -0.5))
        make(G.memset(zeros[:], 0.0))
        make(G.memset(m_full[:], 0.0))
        make(G.memset(ones, 1.0))
        make(G.memset(causal[:], 1))
        make(G.affine_select(out=causal[:], in_=causal[:], compare_op=ALU.is_ge, fill=0, base=0, pattern=[[1, P]],
                             channel_multiplier=-1))
        make(G.affine_select(out=pick[:, 0:1], in_=ones[:, 0:1], compare_op=ALU.is_ge, fill=0.0, base=HALF - 1,
                             pattern=[[0, 1]], channel_multiplier=-1))
        make(G.affine_select(out=pick[:, 1:2], in_=ones[:, 0:1], compare_op=ALU.is_ge, fill=0.0, base=-HALF,
                             pattern=[[0, 1]], channel_multiplier=1))

        def rstd_of(t):
            pool.wait_ge(s["var_ready"], t + 1)
            G.tensor_tensor(rstd[:], var[:], half_neg[:], ALU.pow).then_inc(s["rstd_ready"], 1)

        def scale_bc(t, par, parts=range(3)):
            pool.wait_ge(s["bc_copied"], 2 * (t + 1))
            for i in parts:
                k, n = ((0, P), (1, P), (0, HALF))[i]
                G.tensor_tensor(g[0:n, i, :].rearrange("p (q t) -> p q t", q=SUB),
                                bc[0:n, k, :].rearrange("p (q t) -> p q t", q=SUB),
                                tab[0:n, i, :].unsqueeze(1).broadcast_to([n, SUB, P]), ALU.mult).then_inc(s["g_ready"], 1)

        def rest_of_m(t, par):
            pool.wait_ge(s["m_hi_ready"], t + 1)
            G.tensor_tensor(m_lo[:, par], m_full[:], m_hi[:, par].bitcast(F32), ALU.subtract).then_inc(s["m_lo_ready"], 1)

        def first_tap(t, par, j):
            new_chain()
            settle(pool)
            pool.wait_ge(s["raw_ready"], CT * t + j + 1)
            after(pool, "tap0_ready", CT * t + j)
            before = raw[:, j % 2, 0:TAPS - 1]
            end = raw[:, j % 2, TILE:TILE + TAPS - 1]
            if par == 0:
                link(G.tensor_tensor(carry[:, j, :], end, zeros[:], ALU.add))
                link(G.memset(before, 0.0))
            else:
                link(G.tensor_tensor(before, carry[:, j, :], zeros[:], ALU.add))
                link(G.tensor_copy(carry[:, j, :], end))
            link(G.tensor_scalar(tap0[:], raw[:, j % 2, 0:TILE], taps[:, j, 0:1], None, ALU.mult))
            G.tensor_tensor(xs[:, par, j, :], xs[:, par, j, :], tap0[:], ALU.add).then_inc(s["tap0_ready"], 1)

        pool.wait_ge(s["init_a"], 1)
        G.tensor_scalar(rate[:], rate[:], -1.0, -MAX_RATE, ALU.mult, ALU.max).then_inc(s["rate_ready"], 1)
        rstd_of(0)
        a, b = PIECES[1]
        pool.wait_ge(s["w_hi"], 2)
        G.tensor_tensor(win_lo[:, :, a:b], win_raw[1], win_hi[:, :, a:b].bitcast(F32), ALU.subtract).then_inc(s["w_lo"], 1)
        rstd_of(1)
        pool.wait_ge(s["init_a"], 4)
        pool.wait_ge(s["small_in"], 64)
        pool.wait_ge(s["w_lo_v"], 1)
        for j in range(CT):
            first_tap(0, 0, j)
            if 1 <= j <= 3:
                scale_bc(0, 0, (j - 1,))
        rest_of_m(0, 0)
        pool.wait_ge(s["w_lo_v"], 2)
        pool.wait_ge(s["init_a"], 8)
        first_tap(1, 1, 0)
        pool.wait_ge(s["flag_ready"], 1)
        general = pool.value_load(flag[0:1, 0:1], min_val=0, max_val=1)

        def tile(t, par):
            nx = 1 - par
            for q in range(SUB):
                c = SUB * t + q
                first_tap(t + 1, nx, 2 * q + 1)
                if q == 1:
                    pool.wait_ge(s["res_in"], 16 * (t + 1))
                    G.tensor_tensor(x_res[:], x_res[:], bias_out[:].unsqueeze(1).broadcast_to([P, SUB, D]),
                                    ALU.add).then_inc(s["res_biased"], 1)
                with pool.If(general == 0):
                    pool.wait_ge(s["S_hi_ready"], c + 1)
                    G.tensor_tensor(S_lo[:], S[:], S_hi[:].bitcast(F32), ALU.subtract).then_inc(s["S_lo_ready"], 1)
                if q == 0:
                    scale_bc(t + 1, nx)
                if q == 3:
                    rest_of_m(t + 1, nx)
                pool.wait_ge(s["yvar_ready"], c + 1)
                G.tensor_tensor(yrstd[:], yvar[:], half_neg[:, 0:1], ALU.pow).then_inc(s["yrstd_ready"], 1)
                if q < SUB - 1:
                    first_tap(t + 1, nx, 2 * q + 2)
                else:
                    first_tap(t + 2, par, 0)
                if q == 1:
                    rstd_of(t + 2)

        pairs_of_tiles(pool, tile)

    @block.scalar
    def _(act):
        A = nc.scalar
        act.wait_ge(s["rate_in"], 32)
        A.activation(rate[:], rate[:], ACT.Exp).then_inc(s["init_a"], 1)
        act.wait_ge(s["rate_ready"], 1)
        act.wait_ge(s["init_p"], INIT_P)
        A.activation(tab[:], expo, ACT.Exp, scale=rate[:, 0:1]).then_inc(s["init_a"], 1)
        act.wait_ge(s["init_a"], 2)
        A.mul(tab[0:HALF, 0, HALF:P], ones[0:HALF, 0:HALF], 0.0).then_inc(s["init_a"], 1)
        A.activation(chunk_decay[:], rate[:], ACT.Exp, scale=float(P)).then_inc(s["init_a"], 1)
        act.wait_ge(s["ga_in"], 16)
        A.activation(ga[:], ga[:], ACT.Exp).then_inc(s["init_a"], 1)
        act.wait_ge(s["init_a"], 5)
        A.activation(ga[:], ga[:], ACT.Exp, scale=-1.0).then_inc(s["init_a"], 1)
        act.wait_ge(s["a_in"], 32)
        A.activation(sz[:, NST:2 * NST], sz[:, 0:NST], ACT.Exp).then_inc(s["init_a"], 1)
        for n, (a, b) in enumerate(PIECES):
            act.wait_ge(s[f"w_in{n}"], 16)
            A.copy(win_hi[:, :, a:b], win_raw[n]).then_inc(s["w_hi"], 1)

        def round_xT(t, par):
            act.wait_ge(s["xT_in_psum"], t + 1)
            A.copy(xT_hi[:, par], mm_ps[:]).then_inc(s["xT_hi_ready"], 1)

        def copy_bc(t, par, i):
            act.wait_ge(s["bc_in_psum"], 2 * t + i + 1)
            after(act, "g_ready", 3 * t)
            A.copy(bc[:, i, :], mm_ps[:, i, :]).then_inc(s["bc_copied"], 1)

        def round_g(t, par):
            act.wait_ge(s["g_ready"], 3 * (t + 1))
            A.copy(g1_hi[:, par, :], g[:, 0, :]).then_inc(s["g_hi_ready"], 1)
            A.copy(g23_hi[:, 0, :], g[:, 1, :]).then_inc(s["g_hi_ready"], 1)
            A.copy(g23_hi[0:HALF, 1, :], g[0:HALF, 2, :]).then_inc(s["g_hi_ready"], 1)

        def round_bo(t, par):
            act.wait_ge(s["bo_in_psum"], t + 1)
            A.copy(bo_hi[:, par].rearrange("p q t -> p (q t)"), mm_ps[:, 0, :]).then_inc(s["bo_hi_ready"], 1)

        def round_m(t, par):
            act.wait_ge(s["m_masked"], t + 1)
            A.copy(m_hi[:, par], m_full[:]).then_inc(s["m_hi_ready"], 1)

        def copy_xp(t, par, j):
            act.wait_ge(s["xp_in_psum"], CT * t + j + 1)
            after(act, "conv_done", CT * t + j - 1)
            A.copy(raw[:, j % 2, TAPS - 1:], mm_ps[:, j % 2, :])
            A.activation(xs[:, par, j, :], mm_ps[:, j % 2, :], ACT.Identity, bias=vecs[:, 0, j:j + 1],
                         scale=taps[:, j, TAPS - 1:TAPS]).then_inc(s["raw_ready"], 1)

        def silu_x(t, par, j):
            act.wait_ge(s["conv_done"], CT * t + j + 1)
            A.activation(xs[:, par, j, :], xs[:, par, j, :], ACT.Silu).then_inc(s["xs_ready"], 1)

        def round_ynT(c):
            act.wait_ge(s["yn_in_psum"], c + 1)
            after(act, "out_in_psum", c)
            A.copy(ynT_hi[:].rearrange("p c t -> p (c t)"), zy_ps[:].rearrange("p b t -> p (b t)")).then_inc(s["ynT_hi_ready"], 1)

        def round_X(c):
            act.wait_ge(s["X_in_psum"], c + 1)
            after(act, "y_in_psum", c)
            A.copy(X_hi[:], xu_ps[:].rearrange("p b t -> p (b t)")).then_inc(s["X_hi_ready"], 1)

        def silu_z(c):
            act.wait_ge(s["z_in_psum"], c + 1)
            after(act, "y_gated", c)
            A.activation(sz[:], zy_ps[:].rearrange("p b t -> p (b t)"), ACT.Silu).then_inc(s["z_ready"], 1)

        round_xT(0, 0)
        for i in range(2):
            copy_bc(0, 0, i)
        act.wait_ge(s["small_in"], 64)
        act.wait_ge(s["w_lo"], 1)
        act.wait_ge(s["w_lo_v"], 1)
        copy_xp(0, 0, 0)
        copy_xp(0, 0, 1)
        for j in range(2, CT):
            if j == 2:
                act.wait_ge(s["bias_in_psum"], 1)
                A.copy(bias_out[:], y_ps[:, 0, 0:D]).then_inc(s["init_a"], 1)
            silu_x(0, 0, j - 2)
            copy_xp(0, 0, j)
            if j == 3:
                act.wait_ge(s["init_v"], 2)
                A.copy(wout[:, :, 0, :], wout_raw).then_inc(s["w_hi"], 1)
            if j == 4:
                round_g(0, 0)
        round_bo(0, 0)
        silu_x(0, 0, CT - 2)
        silu_x(0, 0, CT - 1)
        round_m(0, 0)
        round_xT(1, 1)
        round_X(0)
        silu_z(0)
        act.wait_ge(s["w_lo_v"], 2)
        copy_xp(1, 1, 0)
        copy_xp(1, 1, 1)
        act.wait_ge(s["flag_ready"], 1)
        general = act.value_load(flag[0:1, 0:1], min_val=0, max_val=1)

        def tile(t, par):
            nx = 1 - par
            for q in range(SUB):
                c = SUB * t + q
                if not (isinstance(c, int) and c == 0):
                    round_ynT(c - 1)
                if q == 3:
                    round_xT(t + 2, par)
                with act.If(general == 0):
                    act.wait_ge(s["y_in_psum"], c + 1)
                    act.wait_ge(s["S_ready"], c + 1)
                    A.copy(S_hi[:], S[:]).then_inc(s["S_hi_ready"], 1)
                if q == 1:
                    round_g(t + 1, nx)
                silu_x(t + 1, nx, 2 * q)
                if q == 0:
                    with act.If(general == 1):
                        settle(act)
                        act.wait_ge(s["gbc_out"], 16 * (t + 1))
                        copy_bc(t + 1, nx, 0)
                    with act.Else():
                        settle(act)
                        copy_bc(t + 1, nx, 0)
                    copy_bc(t + 1, nx, 1)
                if q == 2:
                    round_bo(t + 1, nx)
                if q < SUB - 1:
                    copy_xp(t + 1, nx, 2 * q + 2)
                else:
                    copy_xp(t + 2, par, 0)
                silu_x(t + 1, nx, 2 * q + 1)
                if q == 2:
                    round_m(t + 1, nx)
                round_X(c + 1)
                silu_z(c + 1)
                if q < SUB - 1:
                    copy_xp(t + 1, nx, 2 * q + 3)
                else:
                    copy_xp(t + 2, par, 1)

        pairs_of_tiles(act, tile)
        round_ynT(SUB * NT - 1)

    @block.vector
    def _(dve):
        V = nc.vector
        links = [0]

        def link(ins):
            links[0] += 1
            ins.then_inc(s["chain"], 1)
            dve.wait_ge(s["chain"], links[0])

        def new_chain():
            dve.sem_clear(s["chain"])
            links[0] = 0

        def statistics(t):
            new_chain()
            dve.wait_ge(s["x_in"], 16 * (t + 1))
            for i in range(SUB):
                link(V.bn_stats(bn[:, i, :], x_ln[:, i, :]))
            for i in range(SUB):
                link(V.bn_aggr(mv[:, i, :], bn[:, i, :]))
            V.tensor_scalar(var[:], mv[:, :, 1], LN_EPS, None, ALU.add).then_inc(s["var_ready"], 1)

        def normalize(t):
            dve.wait_ge(s["rstd_ready"], t + 1)
            after(dve, "xT_in_psum", t)
            for i in range(SUB):
                V.tensor_scalar(xn[:, i, :], x_ln[:, i, :], mv[:, i, 0:1], rstd[:, i:i + 1],
                                ALU.subtract, ALU.mult).then_inc(s["xn_ready"], 1)
            dve.wait_ge(s["xn_ready"], SUB * (t + 1))
            V.memset(bn[:, 0, 0:1], 0.0).then_inc(s["ln_read"], 1)

        def rest_of_xT(t, par):
            dve.wait_ge(s["xT_hi_ready"], t + 1)
            V.tensor_tensor(xT_lo[:, par], mm_ps[:], xT_hi[:, par].bitcast(F32), ALU.subtract).then_inc(s["xT_lo_ready"], 1)

        def rest_of_g(t, par):
            dve.wait_ge(s["g_hi_ready"], 3 * (t + 1))
            for i in range(3):
                gh_, gl_, n = ((g1_hi[:, par, :], g1_lo[:, par, :], P), (g23_hi[:, 0, :], g23_lo[:, 0, :], P),
                               (g23_hi[:, 1, :], g23_lo[:, 1, :], HALF))[i]
                V.tensor_tensor(gl_[0:n], g[0:n, i, :], gh_[0:n].bitcast(F32), ALU.subtract).then_inc(s["g_lo_ready"], 1)

        def rest_of_bo(t, par):
            dve.wait_ge(s["bo_hi_ready"], t + 1)
            V.tensor_tensor(bo_lo[:, par].rearrange("p q t -> p (q t)"), mm_ps[:, 0, :],
                            bo_hi[:, par].rearrange("p q t -> p (q t)").bitcast(F32), ALU.subtract).then_inc(s["bo_lo_ready"], 1)

        def mask_m(t, par):
            settle(dve)
            dve.wait_ge(s["m_in_psum"], t + 1)
            after(dve, "m_lo_ready", t)
            V.copy_predicated(m_full[:], causal[:].unsqueeze(1).broadcast_to([P, SUB, P]),
                              mm_ps[:, 1, :].rearrange("p (q t) -> p q t", q=SUB)).then_inc(s["m_masked"], 1)

        def convolve(t, par, j):
            new_chain()
            dve.wait_ge(s["tap0_ready"], CT * t + j + 1)
            acc = xs[:, par, j, :]
            for k in range(1, TAPS - 1):
                ins = V.scalar_tensor_tensor(out=acc, in0=raw[:, j % 2, k:k + TILE], scalar=taps[:, j, k:k + 1], in1=acc,
                                             op0=ALU.mult, op1=ALU.add)
                if k < TAPS - 2:
                    link(ins)
            ins.then_inc(s["conv_done"], 1)

        def rest_of_ynT(c):
            dve.wait_ge(s["ynT_hi_ready"], c + 1)
            V.tensor_tensor(ynT_lo[:].rearrange("p c t -> p (c t)"), zy_ps[:].rearrange("p b t -> p (b t)"),
                            ynT_hi[:].rearrange("p c t -> p (c t)").bitcast(F32), ALU.subtract).then_inc(s["ynT_lo_ready"], 1)

        def add_out(t, c, q):
            dve.wait_ge(s["out_in_psum"], c + 1)
            dve.wait_ge(s["res_biased"], t + 1)
            V.tensor_tensor(x_res[:, q, :], xu_ps[:, 0, D:2 * D], x_res[:, q, :], ALU.add).then_inc(s["half_added"], 1)
            dve.wait_ge(s["half_added"], c + 1)
            V.tensor_tensor(x_res[:, q, :], xu_ps[:, 0, 0:D], x_res[:, q, :], ALU.add).then_inc(s["out_added"], 1)

        statistics(0)
        normalize(0)
        dve.wait_ge(s["a_in"], 32)
        link(V.tensor_tensor(S[:, 0:CT * NST].rearrange("p (j n) -> p j n", n=NST),
                             S[:, 0:CT * NST].rearrange("p (j n) -> p j n", n=NST),
                             sz[:, 0:NST].unsqueeze(1).broadcast_to([P, CT, NST]), ALU.not_equal))
        link(V.tensor_reduce(flag_f[:, 0:1], S[:, 0:CT * NST], AX.X, ALU.max))
        dve.wait_ge(s["init_a"], 7)
        link(V.tensor_scalar(sz[:, NST:2 * NST], sz[:, NST:2 * NST], MAX_RATE, None, ALU.is_gt))
        link(V.tensor_reduce(flag_f[:, 1:2], sz[:, NST:2 * NST], AX.X, ALU.max))
        V.tensor_tensor(flag_f[:, 0:1], flag_f[:, 0:1], flag_f[:, 1:2], ALU.add).then_inc(s["init_v"], 1)
        dve.wait_ge(s["flag_sum"], 1)
        V.tensor_scalar(flag[:], zy_ps[:, 0, 0:1], 0.5, None, ALU.is_gt).then_inc(s["flag_ready"], 1)
        a, b = PIECES[0]
        dve.wait_ge(s["w_hi"], 1)
        V.tensor_tensor(win_lo[:, :, a:b], win_raw[0], win_hi[:, :, a:b].bitcast(F32), ALU.subtract).then_inc(s["w_lo_v"], 1)
        rest_of_xT(0, 0)
        statistics(1)
        normalize(1)
        for j in range(CT):
            if j == 2:
                dve.wait_ge(s["bias_in_psum"], 1)
                V.tensor_tensor(wout_raw, wout_raw, vecs[:, 1, :].unsqueeze(2).broadcast_to([P, CT, D]),
                                ALU.mult).then_inc(s["init_v"], 1)
            if j == 5:
                dve.wait_ge(s["w_hi"], 3)
                V.tensor_tensor(wout[:, :, 1, :], wout_raw, wout[:, :, 0, :].bitcast(F32), ALU.subtract).then_inc(s["w_lo_v"], 1)
            convolve(0, 0, j)
            if j == 5:
                rest_of_g(0, 0)
        rest_of_bo(0, 0)
        mask_m(0, 0)
        rest_of_xT(1, 1)
        dve.wait_ge(s["flag_ready"], 1)
        general = dve.value_load(flag[0:1, 0:1], min_val=0, max_val=1)

        def rest_of_X(c):
            dve.wait_ge(s["X_hi_ready"], c + 1)
            V.tensor_tensor(X_lo[:], xu_ps[:].rearrange("p b t -> p (b t)"), X_hi[:].bitcast(F32),
                            ALU.subtract).then_inc(s["X_lo_ready"], 1)

        rest_of_X(0)

        def tile(t, par):
            nx = 1 - par
            for q in range(SUB):
                c = SUB * t + q
                start = isinstance(c, int) and c == 0
                first = par == 0 and q == 0
                if not start:
                    rest_of_ynT(c - 1)
                with dve.If(general == 1):
                    new_chain()
                    dve.wait_ge(s["gbc_in"], 16 * (c + 1))
                    link(V.tensor_copy(gb[0:HALF, :], gbc[0:HALF, 0, :]))
                    link(V.tensor_copy(gb[HALF:P, :], gbc[HALF:P, 1, :]))
                    link(V.tensor_copy(gc[0:HALF, :], gbc[0:HALF, 1, :]))
                    link(V.tensor_copy(gc[HALF:P, :], gbc[HALF:P, 0, :]))
                    if first:
                        link(V.memset(gs[:], 0.0))
                    with dve.Fori(0, PAIRS) as pair:
                        dve.sem_clear(s["gchain"])
                        dve.wait_ge(s["gx_in"], 32)
                        dve.sem_clear(s["gx_in"])
                        V.tensor_tensor(gx, gx, gb, ALU.mult).then_inc(s["gchain"], 1)
                        dve.wait_ge(s["gchain"], 1)
                        V.tensor_tensor_scan(gh, ga[:, bass.ds(pair, 1)].broadcast_to([P, P]), gx,
                                             gs[:, bass.ds(pair, 1)], ALU.mult, ALU.add).then_inc(s["gchain"], 1)
                        dve.wait_ge(s["gchain"], 2)
                        V.tensor_copy(gs[:, bass.ds(pair, 1)], gh[:, P - 1:P]).then_inc(s["gchain"], 1)
                        dve.wait_ge(s["gchain"], 3)
                        V.tensor_tensor(gh, gh, gc, ALU.mult).then_inc(s["gh_ready"], 1)
                    V.memset(flag_f[:, 1:2], 0.0).then_inc(s["S_ready"], 1)
                    settle(dve)
                    dve.wait_ge(s["S_ready"], c + 1)
                with dve.Else():
                    dve.wait_ge(s["u_in_psum"], c + 1)
                    after(dve, "S_lo_ready", c)
                    u = xu_ps[:].rearrange("p b t -> p (b t)")
                    if first:
                        V.tensor_copy(S[:], u).then_inc(s["S_ready"], 1)
                    else:
                        V.scalar_tensor_tensor(out=S[:], in0=S[:], scalar=chunk_decay[:, 0:1], in1=u,
                                               op0=ALU.mult, op1=ALU.add).then_inc(s["S_ready"], 1)
                convolve(t + 1, nx, 2 * q)
                if q == 3:
                    rest_of_xT(t + 2, par)
                new_chain()
                dve.wait_ge(s["y_in_psum"], c + 1)
                dve.wait_ge(s["z_ready"], c + 1)
                after(dve, "yn_in_psum", c)
                V.tensor_tensor(yn[:], y_ps[:].rearrange("p b t -> p (b t)"), sz[:], ALU.mult).then_inc(s["y_gated"], 1)
                if q == 2:
                    rest_of_bo(t + 1, nx)
                    mask_m(t + 1, nx)
                convolve(t + 1, nx, 2 * q + 1)
                new_chain()
                dve.wait_ge(s["y_gated"], c + 1)
                link(V.bn_stats(ybn[:, 0, :], yn[:, 0:TILE]))
                if not start:
                    if q:
                        add_out(t, c - 1, q - 1)
                    else:
                        add_out(t - 1, c - 1, SUB - 1)
                link(V.bn_stats(ybn[:, 1, :], yn[:, TILE:2 * TILE]))
                link(V.bn_aggr(ymv[:], ybn[:]))
                V.tensor_scalar(yvar[:], ymv[:, 1:2], LN_EPS, None, ALU.add).then_inc(s["yvar_ready"], 1)
                dve.wait_ge(s["yrstd_ready"], c + 1)
                V.tensor_scalar(yn[:], yn[:], ymv[:, 0:1], yrstd[:, 0:1], ALU.subtract, ALU.mult).then_inc(s["yn_ready"], 1)
                rest_of_X(c + 1)
                if q == 1:
                    rest_of_g(t + 1, nx)
                    statistics(t + 2)
                if q == 2:
                    normalize(t + 2)

        pairs_of_tiles(dve, tile)
        rest_of_ynT(SUB * NT - 1)
        add_out(NT - 1, SUB * NT - 1, SUB - 1)

    @block.tensor
    def _(pe):
        def product(out, w_hi, w_lo, x_hi, x_lo, start, stop):
            nc.tensor.matmul(out, w_hi, x_hi, start=start, stop=False)
            nc.tensor.matmul(out, w_hi, x_lo, start=False, stop=False)
            return nc.tensor.matmul(out, w_lo, x_hi, start=False, stop=stop)

        def transpose_xn(t):
            pe.wait_ge(s["xn_ready"], SUB * (t + 1))
            after(pe, "raw_ready", CT * t)
            for k in range(KT):
                for i in range(SUB):
                    last = nc.tensor.transpose(mm_ps[:, k, i * P:(i + 1) * P], xn[:, i, k * P:(k + 1) * P], ident[:])
            last.then_inc(s["xT_in_psum"], 1)

        def project(out, col, par):
            for k in range(KT):
                last = product(out, win_hi[:, k, col:col + P], win_lo[:, k, col:col + P], xT_hi[:, par, k, :],
                               xT_lo[:, par, k, :], k == 0, k == KT - 1)
            return last

        def project_bc(t, par):
            for i, col in enumerate((COL_BC, COL_CB)):
                if isinstance(t, int) and t == 0:
                    pe.wait_ge(s["xT_lo_ready"], 1)
                else:
                    pe.wait_ge(s["raw_ready"], CT * t + i + 1)
                project(mm_ps[:, i, :], col, par).then_inc(s["bc_in_psum"], 1)

        def project_x(t, par, j, before, count):
            pe.wait_ge(s[before], count)
            project(mm_ps[:, j % 2, :], j * P, par).then_inc(s["xp_in_psum"], 1)

        def decays(t, par):
            pe.wait_ge(s["raw_ready"], CT * t + (CT if isinstance(t, int) and t == 0 else 6))
            pe.wait_ge(s["g_lo_ready"], 3 * (t + 1))
            for q in range(SUB):
                last = nc.tensor.transpose(mm_ps[:, 0, q * P:(q + 1) * P], g[:, 1, q * P:(q + 1) * P], ident[:])
            last.then_inc(s["bo_in_psum"], 1)
            for q in range(SUB):
                a = q * P
                for blk in range(2):
                    b_hi = g1_hi[0:HALF, par, a:a + P] if blk == 0 else g23_hi[0:HALF, 1, a:a + P]
                    b_lo = g1_lo[0:HALF, par, a:a + P] if blk == 0 else g23_lo[0:HALF, 1, a:a + P]
                    t0 = a + blk * HALF
                    last = product(mm_ps[:, 1, t0:t0 + HALF], b_hi, b_lo, g23_hi[0:HALF, 0, t0:t0 + HALF],
                                   g23_lo[0:HALF, 0, t0:t0 + HALF], True, True)
            last.then_inc(s["m_in_psum"], 1)

        def transpose_yn(c):
            pe.wait_ge(s["z_ready"], c + 2)
            pe.wait_ge(s["yn_ready"], c + 1)
            for j in range(CT):
                last = nc.tensor.transpose(zy_ps[:, j // SUB, (j % SUB) * P:(j % SUB + 1) * P], yn[:, j * P:(j + 1) * P], ident[:])
            last.then_inc(s["yn_in_psum"], 1)

        def project_out(c, left):
            pe.wait_ge(s["ynT_lo_ready"], c + 1)
            pe.wait_ge(s[left], c + 2)
            for j in range(CT):
                nc.tensor.matmul(xu_ps[:, 0, :], ynT_hi[:, j, :], wout[:, j].rearrange("p h d -> p (h d)"),
                                 start=(j == 0), stop=False)
                last = nc.tensor.matmul(xu_ps[:, 0, 0:D], ynT_lo[:, j, :], wout[:, j, 0, :], start=False,
                                        stop=(j == CT - 1))
            last.then_inc(s["out_in_psum"], 1)

        def project_z(c, par, q, n):
            if n == 0:
                after(pe, "ynT_lo_ready", c - 1)
            col = COL_Z + n * TILE
            for k in range(KT):
                xh, xl = xT_hi[:, par, k, q * P:(q + 1) * P], xT_lo[:, par, k, q * P:(q + 1) * P]
                last = product(zy_ps[:, n, :], xh, xl, win_hi[:, k, col:col + TILE], win_lo[:, k, col:col + TILE],
                               k == 0, k == KT - 1)
            if n == 1:
                last.then_inc(s["z_in_psum"], 1)

        def transpose_x(t, c, par, q):
            if q == 0:
                pe.wait_ge(s["xs_ready"], CT * (t + 1))
            if isinstance(c, int) and c < 2:
                after(pe, "S_ready", c)
            else:
                pe.wait_ge(s["out_added"], c - 1)
            for j in range(CT):
                last = nc.tensor.transpose(xu_ps[:, j // SUB, (j % SUB) * P:(j % SUB + 1) * P],
                                           xs[:, par, j, q * P:(q + 1) * P], ident[:])
            last.then_inc(s["X_in_psum"], 1)

        pe.wait_ge(consts["ident_ready"], consts["ident_count"])
        transpose_xn(0)
        pe.wait_ge(s["init_v"], 1)
        pe.wait_ge(s["init_p"], INIT_P)
        nc.tensor.matmul(zy_ps[:, 0, 0:1], ones, flag_f[:, 0:1], start=True, stop=True).then_inc(s["flag_sum"], 1)
        pe.wait_ge(s["w_lo_v"], 1)
        project_bc(0, 0)
        pe.wait_ge(s["w_lo"], 1)
        project_x(0, 0, 0, "bc_copied", 1)
        project_x(0, 0, 1, "bc_copied", 2)
        pe.wait_ge(s["w_out"], 16)
        pe.wait_ge(s["small_in"], 64)
        for j in range(CT):
            last = nc.tensor.matmul(y_ps[:, 0, 0:D], vecs[:, 2, j:j + 1].broadcast_to([P, P]), wout_raw[:, j, :],
                                    start=(j == 0), stop=(j == CT - 1))
        last.then_inc(s["bias_in_psum"], 1)
        for j in range(2, CT):
            project_x(0, 0, j, "raw_ready", j - 1)
        decays(0, 0)
        pe.wait_ge(s["bo_lo_ready"], 1)
        pe.wait_ge(s["m_masked"], 1)
        transpose_xn(1)
        pe.wait_ge(s["flag_ready"], 1)
        project_z(0, 0, 0, 0)
        transpose_x(0, 0, 0, 0)
        project_z(0, 0, 0, 1)
        for j in range(2):
            project_x(1, 1, j, "xT_lo_ready", 2)
        pe.wait_ge(s["init_a"], 8)
        pe.wait_ge(s["w_lo_v"], 2)
        general = pe.value_load(flag[0:1, 0:1], min_val=0, max_val=1)

        def tile(t, par):
            nx = 1 - par
            for q in range(SUB):
                c = SUB * t + q
                start = isinstance(c, int) and c == 0
                first = par == 0 and q == 0
                if not start:
                    transpose_yn(c - 1)
                pe.wait_ge(s["X_lo_ready"], c + 1)
                with pe.If(general == 1):
                    nc.tensor.matmul(xu_ps[:, 0, 0:2], ident[:], pick[:], start=True, stop=True).then_inc(s["u_in_psum"], 1)
                with pe.Else():
                    if q == 0:
                        pe.wait_ge(s["bo_lo_ready"], t + 1)
                    for n in range(2):
                        cols = slice(n * TILE, (n + 1) * TILE)
                        last = product(xu_ps[:, n, :], bo_hi[:, par, q, :], bo_lo[:, par, q, :], X_hi[:, cols], X_lo[:, cols],
                                       True, True)
                    last.then_inc(s["u_in_psum"], 1)
                if q == 3:
                    transpose_xn(t + 2)
                after(pe, "y_gated", c)
                with pe.If(general == 1):
                    with pe.Fori(0, PAIRS) as pair:
                        pe.wait_ge(s["gh_ready"], 1)
                        pe.sem_clear(s["gh_ready"])
                        nc.tensor.matmul(y_ps[:].rearrange("p b t -> p (b t)")[:, bass.ds(pair * 2, 2)], gh, pick[:],
                                         start=True, stop=True).then_inc(s["pair_done"], 1)
                    nc.tensor.matmul(y_ps[:, 1, TILE - 2:TILE], gh, pick[:], start=True, stop=True).then_inc(s["y_in_psum"], 1)
                with pe.Else():
                    if q == 0:
                        pe.wait_ge(s["m_lo_ready"], t + 1)
                    if not first:
                        pe.wait_ge(s["S_lo_ready"], c)
                    for n in range(2):
                        cols = slice(n * TILE, (n + 1) * TILE)
                        last = product(y_ps[:, n, :], m_hi[:, par, q, :], m_lo[:, par, q, :], X_hi[:, cols], X_lo[:, cols],
                                       True, first)
                        if not first:
                            ca = slice(q * P, (q + 1) * P)
                            last = product(y_ps[:, n, :], g1_hi[HALF:P, par, ca], g1_lo[HALF:P, par, ca],
                                           S_hi[HALF:P, cols], S_lo[HALF:P, cols], False, True)
                    last.then_inc(s["y_in_psum"], 1)
                if q == 0:
                    project_bc(t + 1, nx)
                    project_x(t + 1, nx, 2, "bc_copied", 2 * (t + 1) + 1)
                if q == 1:
                    project_x(t + 1, nx, 4, "raw_ready", CT * (t + 1) + 3)
                if q == 2:
                    decays(t + 1, nx)
                    project_x(t + 1, nx, 6, "bo_lo_ready", t + 2)
                if q == 3:
                    project_x(t + 2, par, 0, "xT_lo_ready", t + 3)
                if not start:
                    project_out(c - 1, "S_ready")
                nt, npar, nq = (t, par, q + 1) if q < SUB - 1 else (t + 1, nx, 0)
                project_z(c + 1, npar, nq, 0)
                transpose_x(nt, c + 1, npar, nq)
                project_z(c + 1, npar, nq, 1)
                if q == 0:
                    project_x(t + 1, nx, 3, "bc_copied", 2 * (t + 1) + 2)
                if q == 1:
                    project_x(t + 1, nx, 5, "raw_ready", CT * (t + 1) + 4)
                if q == 2:
                    project_x(t + 1, nx, 7, "m_masked", t + 2)
                if q == 3:
                    project_x(t + 2, par, 1, "xT_lo_ready", t + 3)

        pairs_of_tiles(pe, tile)
        transpose_yn(SUB * NT - 1)
        project_out(SUB * NT - 1, "X_lo_ready")


def program(nc, x, in_proj, out_proj, conv_w, conv_b, ln_w, ln_b, A, A_pairs, gate_up, down, router, e_bias, out):
    def scratch(name, shape):
        return nc.dram_tensor(name, shape, F32, kind="Internal").ap()

    x1, x2 = scratch("x1", [TOK, D]), scratch("x2", [TOK, D])
    ffn_w = dict(gate_up=gate_up, down=down, router=router, e_bias=e_bias)
    attn_w = dict(in_proj=in_proj, out_proj=out_proj, conv_w=conv_w, conv_b=conv_b, ln_w=ln_w, ln_b=ln_b, A=A,
                  A_pairs=A_pairs)
    with ExitStack() as whole:
        ident = whole.enter_context(nc.sbuf_tensor("ident", [P, P], F32))
        ident_ready = whole.enter_context(nc.semaphore("ident_ready"))
        nc.gpsimd.memset(ident[:], 0.0).then_inc(ident_ready, 1)
        nc.gpsimd.wait_ge(ident_ready, 1)
        nc.gpsimd.affine_select(out=ident[:], in_=ident[:], compare_op=ALU.not_equal, fill=1.0, base=0,
                                pattern=[[-1, P]], channel_multiplier=1).then_inc(ident_ready, 1)
        consts = dict(ident=ident, ident_ready=ident_ready, ident_count=2)
        with ExitStack() as ctx:
            ffn_block(nc, ctx, whole, consts, "f1", x, x1, scratch("rows1", [2 * P, P]), ffn_w)
        with ExitStack() as ctx:
            attn_block(nc, ctx, whole, consts, "at", x1, x2,
                       dict(x_rows=scratch("x_rows", [DI, P]), bc_rows=scratch("bc_rows", [2, P, 2, TILE])), attn_w)
        with ExitStack() as ctx:
            ffn_block(nc, ctx, whole, consts, "f2", x2, out, scratch("rows2", [2 * P, P]), ffn_w)


def kernel(**inputs):
    import numpy as np
    import concourse.bacc as bacc
    from concourse.bass_utils import run_bass_kernel_spmd

    i = {name: np.asarray(a) for name, a in inputs.items()}

    def channels(name):
        a = i[name].reshape(CT, P, -1).transpose(1, 0, 2)
        return a if a.shape[2] > 1 else a[:, :, 0]

    attn, ffn = "L0_attn_", "L0_ffn_"
    w_in = i[attn + "in_proj_w"]
    w_in = np.concatenate([w_in, w_in[COL_BC + NST:COL_BC + 2 * NST], w_in[COL_BC:COL_BC + NST]])
    halves = (SH, P, D)
    gate = np.concatenate([i[ffn + "sh_gate_w"].reshape(halves), i[ffn + "gate_w"]])
    up = np.concatenate([i[ffn + "sh_up_w"].reshape(halves), i[ffn + "up_w"]])
    down = np.concatenate([i[ffn + "sh_down_w"].reshape(D, SH, P).transpose(1, 0, 2), i[ffn + "down_w"]])
    arrays = dict(
        x=i[attn + "x"].reshape(TOK, D),
        in_proj=w_in.reshape(NCOL, KT, P).transpose(2, 1, 0),
        out_proj=i[attn + "out_proj_w"].reshape(D, CT, P).transpose(2, 1, 0),
        conv_w=channels(attn + "conv_w"),
        conv_b=channels(attn + "conv_b"),
        ln_w=channels(attn + "ln_w"),
        ln_b=channels(attn + "ln_b"),
        A=i[attn + "A_param"].reshape(DI, NST),
        A_pairs=i[attn + "A_param"].reshape(PAIRS, P).T,
        gate_up=np.stack([gate, up], 1).reshape(NU, 2, P, KT, P).transpose(4, 0, 3, 1, 2).reshape(P, NU, 2 * D),
        down=down.transpose(2, 0, 1),
        router=i[ffn + "router_weight"].reshape(E, KT, P).transpose(2, 1, 0),
        e_bias=i[ffn + "e_bias"],
    )
    nc = bacc.Bacc("TRN2", target_bir_lowering=False, num_devices=1)
    args, data = [], {}
    for name, a in arrays.items():
        data[f"in_{name}"] = np.ascontiguousarray(a)
        args.append(nc.dram_tensor(f"in_{name}", a.shape, mybir.dt.from_np(a.dtype), kind="ExternalInput").ap())
    args.append(nc.dram_tensor("out", (TOK, D), F32, kind="ExternalOutput").ap())
    program(nc, *args)
    result = run_bass_kernel_spmd(nc, [data], core_ids=[0])
    return result.results[0]["out"].reshape(i[attn + "x"].shape)
```
